# Optimizing a Trainium2 kernel written in Bass

```python
import numpy as np
import jax
import jax.numpy as jnp

def _softmax(x, axis=-1):
    return jax.nn.softmax(x, axis=axis)

def _gelu(x):
    return jax.nn.gelu(x, approximate=True)

def _silu(x):
    return jax.nn.silu(x)

def _sigmoid(x):
    return jax.nn.sigmoid(x)

def _layernorm(x, axis=-1, eps=1e-05):
    m = jnp.mean(x, axis=axis, keepdims=True)
    v = jnp.var(x, axis=axis, keepdims=True)
    return (x - m) / jnp.sqrt(v + eps)

def _scatter_add(tgt, idx, src, axis=0):
    return tgt.at[idx].add(src)

def _segment_sum(src, seg, n):
    return jax.ops.segment_sum(src, seg, n)
kernel_name = 'mk_prb_d1_jaxref_r4_c24616'

def setup_inputs(seed: int=0):
    np.random.seed(seed)
    _w = jnp.asarray

    def _L0_attn_setup():
        import jax, jax.numpy as jnp
        import numpy as np
        from functools import partial
        B, T, C = (4, 512, 512)
        H = C
        LAYER_IDX, TOTAL_LAYERS = (12, 24)

        def wkv_v4(k, v, w, u):
            w_eff = -jnp.exp(w)
            kT = jnp.swapaxes(k, 0, 1)
            vT = jnp.swapaxes(v, 0, 1)
            Bn, Hn = (k.shape[0], k.shape[2])
            aa = jnp.zeros((Bn, Hn), k.dtype)
            bb = jnp.zeros((Bn, Hn), k.dtype)
            pp = jnp.full((Bn, Hn), -1e+38, k.dtype)

            def step(carry, kv_t):
                aa, bb, pp = carry
                kt, vt = kv_t
                ww = u + kt
                p = jnp.maximum(pp, ww)
                e1 = jnp.exp(pp - p)
                e2 = jnp.exp(ww - p)
                y = (e1 * aa + e2 * vt) / (e1 * bb + e2)
                ww2 = w_eff + pp
                p2 = jnp.maximum(ww2, kt)
                e1b = jnp.exp(ww2 - p2)
                e2b = jnp.exp(kt - p2)
                return ((e1b * aa + e2b * vt, e1b * bb + e2b, p2), y)
            _, yT = jax.lax.scan(step, (aa, bb, pp), (kT, vT))
            return jnp.swapaxes(yT, 0, 1)
        key = jax.random.key(seed)
        ks = jax.random.split(key, 8)
        x = jax.random.normal(ks[0], (B, T, C), dtype=jnp.float32)
        li, tl = (float(LAYER_IDX), float(TOTAL_LAYERS))
        ar_c = jnp.arange(C, dtype=jnp.float32)
        mu_k = (ar_c / C) ** (1.0 - li / tl)
        mu_r = mu_k / 2.0
        mu_v = mu_k + 0.3 * li / (tl - 1.0)
        ar_h = jnp.arange(H, dtype=jnp.float32)
        wkv_w = -5.0 + 8.0 * (ar_h / (H - 1)) ** (0.7 + 1.3 * li / (tl - 1.0))
        wkv_u = 0.5 * ((jnp.arange(1, H + 1) % 3).astype(jnp.float32) - 1.0) + jnp.log(0.3)
        s = 1.0 / np.sqrt(C)
        Wr = jax.random.normal(ks[1], (H, C), jnp.float32) * s
        Wk = jax.random.normal(ks[2], (H, C), jnp.float32) * s
        Wv = jax.random.normal(ks[3], (H, C), jnp.float32) * s
        Wo = jax.random.normal(ks[4], (C, H), jnp.float32) * s
        return {'x': x, 'mu_r': mu_r, 'mu_k': mu_k, 'mu_v': mu_v, 'wkv_w': wkv_w, 'wkv_u': wkv_u, 'Wr': Wr, 'Wk': Wk, 'Wv': Wv, 'Wo': Wo}
    _L0_attn_in = _L0_attn_setup()

    def _L0_ffn_setup():
        import jax, jax.numpy as jnp
        import numpy as np
        B, S, D, H = (4, 512, 512, 2048)

        def fwht(x):
            orig_shape = x.shape
            n = orig_shape[-1]
            x = x.reshape(-1, n)
            h = 1
            while h < n:
                xb = x.reshape(-1, n // (2 * h), 2, h)
                a = xb[:, :, 0, :]
                b = xb[:, :, 1, :]
                x = jnp.stack([a + b, a - b], axis=2).reshape(-1, n)
                h *= 2
            scale = jnp.asarray(1.0 / np.sqrt(n), dtype=x.dtype)
            return (x * scale).reshape(orig_shape)
        key = jax.random.key(seed)
        kx, k1, k2, k3 = jax.random.split(key, 4)
        x = jax.random.normal(kx, (B, S, D), dtype=jnp.float32)
        W1 = jax.random.normal(k1, (H, D), dtype=jnp.float32) * (1.0 / np.sqrt(D))
        W2 = jax.random.normal(k2, (D, H), dtype=jnp.float32) * (1.0 / np.sqrt(H))
        W3 = jax.random.normal(k3, (H, D), dtype=jnp.float32) * (1.0 / np.sqrt(D))
        return {'x': x, 'W1': W1, 'W2': W2, 'W3': W3}
    _L0_ffn_in = _L0_ffn_setup()
    _d = {'L0_attn_x': _L0_attn_in['x'], 'L0_attn_mu_r': _L0_attn_in['mu_r'], 'L0_attn_mu_k': _L0_attn_in['mu_k'], 'L0_attn_mu_v': _L0_attn_in['mu_v'], 'L0_attn_wkv_w': _L0_attn_in['wkv_w'], 'L0_attn_wkv_u': _L0_attn_in['wkv_u'], 'L0_attn_Wr': _L0_attn_in['Wr'], 'L0_attn_Wk': _L0_attn_in['Wk'], 'L0_attn_Wv': _L0_attn_in['Wv'], 'L0_attn_Wo': _L0_attn_in['Wo'], 'L0_ffn_W1': _L0_ffn_in['W1'], 'L0_ffn_W2': _L0_ffn_in['W2'], 'L0_ffn_W3': _L0_ffn_in['W3']}
    _x0 = _d['L0_attn_x']
    _d['L0_attn_x'] = jax.random.normal(jax.random.fold_in(jax.random.key(seed), 1), (4, 2048, 512), dtype=_x0.dtype)
    del _x0
    return _d

def reference(L0_attn_x, L0_attn_mu_r, L0_attn_mu_k, L0_attn_mu_v, L0_attn_wkv_w, L0_attn_wkv_u, L0_attn_Wr, L0_attn_Wk, L0_attn_Wv, L0_attn_Wo, L0_ffn_W1, L0_ffn_W2, L0_ffn_W3):

    def _L0_attn_ref(x, mu_r, mu_k, mu_v, wkv_w, wkv_u, Wr, Wk, Wv, Wo):
        import jax, jax.numpy as jnp
        import numpy as np
        from functools import partial
        B, T, C = (4, 512, 512)
        H = C
        LAYER_IDX, TOTAL_LAYERS = (12, 24)

        def wkv_v4(k, v, w, u):
            w_eff = -jnp.exp(w)
            kT = jnp.swapaxes(k, 0, 1)
            vT = jnp.swapaxes(v, 0, 1)
            Bn, Hn = (k.shape[0], k.shape[2])
            aa = jnp.zeros((Bn, Hn), k.dtype)
            bb = jnp.zeros((Bn, Hn), k.dtype)
            pp = jnp.full((Bn, Hn), -1e+38, k.dtype)

            def step(carry, kv_t):
                aa, bb, pp = carry
                kt, vt = kv_t
                ww = u + kt
                p = jnp.maximum(pp, ww)
                e1 = jnp.exp(pp - p)
                e2 = jnp.exp(ww - p)
                y = (e1 * aa + e2 * vt) / (e1 * bb + e2)
                ww2 = w_eff + pp
                p2 = jnp.maximum(ww2, kt)
                e1b = jnp.exp(ww2 - p2)
                e2b = jnp.exp(kt - p2)
                return ((e1b * aa + e2b * vt, e1b * bb + e2b, p2), y)
            _, yT = jax.lax.scan(step, (aa, bb, pp), (kT, vT))
            return jnp.swapaxes(yT, 0, 1)
        shifted = jnp.pad(x, ((0, 0), (1, 0), (0, 0)))[:, :-1]
        xr = mu_r * x + (1.0 - mu_r) * shifted
        xk = mu_k * x + (1.0 - mu_k) * shifted
        xv = mu_v * x + (1.0 - mu_v) * shifted
        r = jnp.einsum('btc,hc->bth', xr, Wr)
        k = jnp.einsum('btc,hc->bth', xk, Wk)
        v = jnp.einsum('btc,hc->bth', xv, Wv)
        wkv = wkv_v4(k, v, wkv_w, wkv_u)
        return jnp.einsum('bth,ch->btc', jax.nn.sigmoid(r) * wkv, Wo)

    def _L0_ffn_ref(x, W1, W2, W3):
        import jax, jax.numpy as jnp
        import numpy as np
        B, S, D, H = (4, 512, 512, 2048)

        def fwht(x):
            orig_shape = x.shape
            n = orig_shape[-1]
            x = x.reshape(-1, n)
            h = 1
            while h < n:
                xb = x.reshape(-1, n // (2 * h), 2, h)
                a = xb[:, :, 0, :]
                b = xb[:, :, 1, :]
                x = jnp.stack([a + b, a - b], axis=2).reshape(-1, n)
                h *= 2
            scale = jnp.asarray(1.0 / np.sqrt(n), dtype=x.dtype)
            return (x * scale).reshape(orig_shape)
        up_gate = jnp.einsum('bsd,hd->bsh', x, W1)
        up_lin = jnp.einsum('bsd,hd->bsh', x, W3)
        hidden = jax.nn.silu(up_gate) * up_lin
        hidden = fwht(hidden)
        out = jnp.einsum('bsh,dh->bsd', hidden, W2)
        return out
    x = L0_attn_x
    xn = _layernorm(x, axis=-1)
    x = x + _L0_attn_ref(xn, L0_attn_mu_r, L0_attn_mu_k, L0_attn_mu_v, L0_attn_wkv_w, L0_attn_wkv_u, L0_attn_Wr, L0_attn_Wk, L0_attn_Wv, L0_attn_Wo) + _L0_ffn_ref(xn, L0_ffn_W1, L0_ffn_W2, L0_ffn_W3)
    return x

_drawn_inputs = setup_inputs


def setup_inputs(seed=0):
    import zlib

    import numpy as np

    out = dict(_drawn_inputs(seed))
    spreads = {}
    factors = {'L0_attn_mu_r': 3.509, 'L0_attn_wkv_u': 64.0}
    for name, (base, spread) in spreads.items():
        noise = np.random.default_rng([zlib.crc32(name.encode()), seed]).standard_normal(out[name].shape)
        drawn = base * np.exp(spread * noise) if base else spread * noise
        out[name] = jnp.asarray(drawn.astype(out[name].dtype))
    for name, factor in factors.items():
        out[name] = (out[name] * factor).astype(out[name].dtype)
    return out
```

```python
from contextlib import ExitStack

import concourse.bass as bass
import numpy as np
from concourse import mybir

B, T, C, H = 4, 2048, 512, 2048
P = 128
N = 512
CHUNKS = B * T // N
CHUNKS_PER_ROW = T // N
KT = C // P
TT = N // P
FT = H // P
EPS = 1e-5
START = -1e38

LAG = 2
RESIDENT = 14
RING = 5
MIX_AHEAD = 3
HID_SLOTS = 3
FLIP_AT = 12


def unit_order():
    order = [(q, kt) for q in ("k", "v", "r") for kt in range(KT)]
    for j in range(FT):
        order += [("w1", j), ("w3", j)]
        if j >= LAG:
            order.append(("w2", j - LAG))
        c, stage = divmod(j - 6, 4)
        if stage == 0 and c >= 0:
            order.append(("wo", c))
    order += [("w2", j) for j in range(FT - LAG, FT)]
    order.append(("wo", KT - 1))
    return order


UNITS = unit_order()
UNIT_AT = {u: n for n, u in enumerate(UNITS)}
NU = len(UNITS)
IS_RESIDENT = [(n + 1) * RESIDENT // NU > n * RESIDENT // NU for n in range(NU)]
RESIDENT_AT = {u: sum(IS_RESIDENT[:n]) for n, u in enumerate(UNITS) if IS_RESIDENT[n]}
STREAMED = [u for n, u in enumerate(UNITS) if not IS_RESIDENT[n]]
STREAMED_AT = {u: n for n, u in enumerate(STREAMED)}
TURNS = len(STREAMED) // RING
assert len(STREAMED) % RING == 0


def build(nc, x, w_units, vectors, hadamard, identity, out):
    f32, f32r = mybir.dt.float32, mybir.dt.float32r
    ALU, ACT = mybir.AluOpType, mybir.ActivationFunctionType

    split = nc.dram_tensor("split_units", [NU, P, 2 * C], f32, kind="Internal").ap()
    x_v = x.rearrange("(s t p) c -> s p t c", t=TT, p=P)
    out_v = out.rearrange("(s t p) c -> s p t c", t=TT, p=P)

    ctx = ExitStack()
    with ctx:
        def sb(name, shape, dt=f32, stack=ctx):
            return stack.enter_context(nc.sbuf_tensor(name, shape, dt))

        def sem(name):
            return ctx.enter_context(nc.semaphore(name))

        resident = [sb(f"resident{i}", [P, 2, C], f32r) for i in range(RESIDENT)]
        ident = sb("ident", [P, P])
        vec = sb("vec", [P, 5, KT])
        one_less_mu = sb("one_less_mu", [P, 3, KT])
        decay = sb("decay", [P, KT])
        keep = sb("keep", [P, CHUNKS + 1])
        keep3 = sb("keep3", [P, 3 * (CHUNKS + 1)])
        reset3 = sb("reset3", [P, 3 * (CHUNKS + 1)])
        half = sb("half", [P, TT])
        carry = sb("carry", [P, KT, 3])
        banks = [ctx.enter_context(nc.psum_tensor(f"bank{i}", [P, N], f32)) for i in range(4)]
        acc = [ctx.enter_context(nc.psum_tensor(f"acc{i}", [P, C], f32)) for i in range(TT)]

        prepare_weights(nc, w_units, hadamard, split, resident, banks, acc)

        ring = [sb(f"ring{i}", [P, 2, C], f32r) for i in range(RING)]
        xn = sb("xn", [P, TT, C])
        xt = sb("xt", [P, KT, N + 1])
        xs = sb("xs", [P, 2, KT, N], f32r)
        mixf = [sb(f"mixf{i}", [P, N]) for i in range(MIX_AHEAD)]
        mix = [sb(f"mix{i}", [P, 2, N], f32r) for i in range(MIX_AHEAD)]
        kvr = sb("kvr", [P, 3, KT, N])
        pab = sb("pab", [P, 3, N + 1])
        tmp = [sb(f"tmp{i}", [P, N]) for i in range(7)]
        att = [sb(f"att{i}", [P, 2, N], f32r) for i in range(2)]
        hidf = [sb(f"hidf{i}", [P, N]) for i in range(HID_SLOTS)]
        hid = [sb(f"hid{i}", [P, 2, N], f32r) for i in range(HID_SLOTS)]
        res = sb("res", [P, TT, C])
        stats = sb("stats", [P, TT, 6])
        mean_var = sb("mean_var", [P, TT, 2])
        var_eps = sb("var_eps", [P, TT])
        rstd = sb("rstd", [P, TT])
        carry_kept = sb("carry_kept", [P, 3])

        per = {}

        def counted(name, n):
            s = sem(name)
            per[s.name] = n
            return s

        const_loaded = sem("const_loaded")
        const_made = sem("const_made")
        decay_made = sem("decay_made")
        x_loaded = counted("x_loaded", 16)
        res_loaded = counted("res_loaded", 16)
        out_stored = counted("out_stored", 16)
        slot_loaded = [counted(f"slot_loaded{i}", 16 * TURNS) for i in range(RING)]
        unit_done = counted("unit_done", NU)
        rkv_bank = counted("rkv_bank", 9)
        xt_psum = counted("xt_psum", KT)
        acc_tile = counted("acc_tile", TT - 1)
        kvr_ready = counted("kvr_ready", 12)
        mix_prev = counted("mix_prev", 12)
        mix_hi = counted("mix_hi", 12)
        xs_hi = counted("xs_hi", KT)
        xt_copied = counted("xt_copied", KT)
        wkv_exp = counted("wkv_exp", 16)
        gate_tanh = counted("gate_tanh", FT)
        hid_hi = counted("hid_hi", FT)
        att_hi = counted("att_hi", KT)
        mix_full = counted("mix_full", 12)
        mix_lo = counted("mix_lo", 12)
        xs_lo = counted("xs_lo", KT)
        exp_arg = counted("exp_arg", 16)
        hid_full = counted("hid_full", FT)
        hid_lo = counted("hid_lo", FT)
        att_full = counted("att_full", KT)
        att_lo = counted("att_lo", KT)
        out_ready = counted("out_ready", TT)
        var_ready = counted("var_ready", 1)
        xn_ready = counted("xn_ready", TT)
        shift_ready = counted("shift_ready", 1)
        vec_step = sem("vec_step")
        rstd_ready = counted("rstd_ready", 1)

        def wait(eng, s, t, k):
            value = t * per[s.name] + k
            if not isinstance(value, int) or value > 0:
                eng.wait_ge(s, value)

        def wait_unit(eng, t, unit):
            wait(eng, unit_done, t, UNIT_AT[unit] + 1)

        def wait_item(eng, t, n):
            wait(eng, unit_done, t, n + 1 if n >= 0 else n + 13 - NU)

        block = ctx.enter_context(nc.Block())

        def over_chunks(eng, chunk):
            chunk(0)
            with eng.Fori(1, CHUNKS - 1) as t:
                chunk(t)
            chunk(CHUNKS - 1)

        def is_last(t):
            return isinstance(t, int) and t == CHUNKS - 1

        @block.sync
        def _(sp):
            sp.dma_start(ident[:, :], identity).then_inc(const_loaded, 16)
            sp.dma_start(vec[:, :, :], vectors).then_inc(const_loaded, 16)
            sp.dma_start(xn[:, :, :], x_v[0]).then_inc(x_loaded, 16)

            def store(t):
                wait(sp, out_ready, t, TT)
                sp.dma_start(out_v[t] if isinstance(t, int) else
                             out[bass.ds(t * N, N), :].rearrange("(t p) c -> p t c", p=P),
                             res[:, :, :]).then_inc(out_stored, 16)

            def rows(t):
                return x[bass.ds(t * N, N), :].rearrange("(t p) c -> p t c", p=P)

            def chunk(t):
                for n, unit in enumerate(STREAMED):
                    before = STREAMED[n - RING]
                    wait(sp, unit_done, t, UNIT_AT[before] + 1 - (NU if n < RING else 0))
                    sp.dma_start(ring[n % RING][:, :, :].bitcast(f32),
                                 split[UNIT_AT[unit]].rearrange("p (a c) -> p a c", a=2))\
                        .then_inc(slot_loaded[n % RING], 16)
                    if n == 4 and not is_last(t):
                        wait(sp, xt_psum, t, KT)
                        sp.dma_start(xn[:, :, :], rows(t + 1)).then_inc(x_loaded, 16)
                    if n == 9 and not (isinstance(t, int) and t == 0):
                        store(t - 1)
                    if n == 20:
                        wait(sp, out_stored, t - 1, 16)
                        sp.dma_start(res[:, :, :], rows(t)).then_inc(res_loaded, 16)

            over_chunks(sp, chunk)
            store(CHUNKS - 1)
            wait(sp, out_stored, CHUNKS - 1, 16)

        @block.gpsimd
        def _(pool):
            def inverse_root(t):
                wait(pool, var_ready, t, 1)
                pool.tensor_tensor(rstd[:, :], var_eps[:, :], half[:, :], ALU.pow).then_inc(rstd_ready, 1)

            pool.wait_ge(const_made, 1)
            inverse_root(0)
            inverse_root(1)
            with pool.Fori(2, CHUNKS) as t:
                inverse_root(t)

        @block.tensor
        def _(pe):
            def weights(t, unit):
                if unit in RESIDENT_AT:
                    return resident[RESIDENT_AT[unit]]
                n = STREAMED_AT[unit]
                wait(pe, slot_loaded[n % RING], t, 16 * (n // RING + 1))
                return ring[n % RING]

            def transposes(t, kts, into):
                wait(pe, xn_ready, t, TT)
                for kt in kts:
                    for tt in range(TT):
                        last = pe.transpose(banks[into + kt % 2][:, tt * P:(tt + 1) * P],
                                            xn[:, tt, kt * P:(kt + 1) * P], ident[:, :])
                    last.then_inc(xt_psum, 1)

            def rkv_item(t, n):
                q, kt = divmod(n, KT)
                w = weights(t, UNITS[n])
                m_in = mix[n % MIX_AHEAD]
                wait(pe, mix_hi, t, n + 1)
                wait(pe, mix_lo, t, n + 1)
                for m in range(KT):
                    if kt == 0:
                        if q == 0 and m % 2 == 0:
                            wait(pe, hid_full, t - 1, FT - 1 + m // 2)
                        elif q:
                            wait(pe, kvr_ready, t, KT * (q - 1) + m + 1)
                    col = slice(m * P, (m + 1) * P)
                    pe.matmul(banks[m][:, :], w[:, 0, col], m_in[:, 0, :], start=kt == 0, stop=False)
                    pe.matmul(banks[m][:, :], w[:, 1, col], m_in[:, 0, :], start=False, stop=False)
                    last = pe.matmul(banks[m][:, :], w[:, 0, col], m_in[:, 1, :], start=False,
                                     stop=kt == KT - 1)
                    if m == KT - 1:
                        last.then_inc(unit_done, 1)
                    elif kt == KT - 1:
                        last.then_inc(rkv_bank, 1)

            def up(t, j):
                b = 2 * (j % 2)
                if j == 0:
                    wait(pe, kvr_ready, t, 10)
                    wait(pe, xs_hi, t, KT)
                    wait(pe, xs_lo, t, KT)
                elif j == 1:
                    wait(pe, kvr_ready, t, 12)
                else:
                    wait(pe, hid_full, t, j - 1)
                if j in (FLIP_AT + 1, FLIP_AT + 2) and not is_last(t):
                    wait(pe, xt_copied, t + 1, 2 * (j - FLIP_AT))
                for n, name in enumerate(("w1", "w3")):
                    w = weights(t, (name, j))
                    for kt in range(KT):
                        col = slice(kt * P, (kt + 1) * P)
                        pe.matmul(banks[b + n][:, :], w[:, 0, col], xs[:, 0, kt, :], start=kt == 0, stop=False)
                        pe.matmul(banks[b + n][:, :], w[:, 1, col], xs[:, 0, kt, :], start=False, stop=False)
                        last = pe.matmul(banks[b + n][:, :], w[:, 0, col], xs[:, 1, kt, :], start=False,
                                         stop=kt == KT - 1)
                    last.then_inc(unit_done, 1)

            def down(t, unit, a, first=False, final=False):
                w = weights(t, unit)
                for tt in range(TT):
                    col = slice(tt * P, (tt + 1) * P)
                    if first:
                        wait(pe, out_ready, t - 1, tt + 1)
                    pe.matmul(acc[tt][:, :], a[:, 0, col], w[:, 0, :], start=first, stop=False)
                    pe.matmul(acc[tt][:, :], a[:, 1, col], w[:, 0, :], start=False, stop=False)
                    last = pe.matmul(acc[tt][:, :], a[:, 0, col], w[:, 1, :], start=False, stop=final)
                    if tt == TT - 1:
                        last.then_inc(unit_done, 1)
                    elif final:
                        last.then_inc(acc_tile, 1)

            def ffn_down(t, j):
                wait(pe, hid_hi, t, j + 1)
                wait(pe, hid_lo, t, j + 1)
                down(t, ("w2", j), hid[j % HID_SLOTS], first=j == 0)

            def att_down(t, c):
                wait(pe, att_hi, t, c + 1)
                wait(pe, att_lo, t, c + 1)
                down(t, ("wo", c), att[c % 2], final=c == KT - 1)

            def chunk(t):
                for n in range(12):
                    rkv_item(t, n)
                for j in range(FT):
                    up(t, j)
                    if j in (FLIP_AT, FLIP_AT + 1) and not is_last(t):
                        wait(pe, hid_full, t, j)
                        transposes(t + 1, (0, 1) if j == FLIP_AT else (2, 3), 2 - 2 * (j % 2))
                    if j >= LAG:
                        ffn_down(t, j - LAG)
                    if ("wo", (j - 6) // 4) in UNIT_AT and (j - 6) % 4 == 0 and j >= 6:
                        att_down(t, (j - 6) // 4)
                for j in range(FT - LAG, FT):
                    ffn_down(t, j)
                att_down(t, KT - 1)

            pe.wait_ge(const_loaded, 32)
            transposes(0, (0, 1), 2)
            transposes(0, (2, 3), 0)
            over_chunks(pe, chunk)

        @block.scalar
        def _(act):
            def mix_first(t, n):
                q, kt = divmod(n, KT)
                if n == 0:
                    wait(act, xt_copied, t, KT)
                    wait(act, shift_ready, t, 1)
                wait(act, mix_lo, t, n + 1 - MIX_AHEAD)
                act.activation(mixf[n % MIX_AHEAD][:, :], xt[:, kt, 0:N], ACT.Copy,
                               scale=one_less_mu[:, q, kt:kt + 1]).then_inc(mix_prev, 1)

            def mix_second(t, n):
                wait(act, mix_full, t, n + 1)
                wait_item(act, t, n - MIX_AHEAD)
                act.activation(mix[n % MIX_AHEAD][:, 0, :], mixf[n % MIX_AHEAD][:, :],
                               ACT.Copy).then_inc(mix_hi, 1)

            def evacuate(t, q):
                for m in range(KT):
                    if m < KT - 1:
                        wait(act, rkv_bank, t, 3 * q + m + 1)
                    else:
                        wait_item(act, t, 4 * q + 3)
                    if q == 0 and m == 0:
                        wait(act, att_full, t - 1, KT)
                    act.activation(kvr[:, q, m, :], banks[m][:, :], ACT.Tanh if q == 2 else ACT.Copy,
                                   scale=0.5 if q == 2 else 1.0).then_inc(kvr_ready, 1)

            def copy_xt(t, kts, bank):
                wait(act, shift_ready, t, 1)
                for kt in kts:
                    wait(act, xt_psum, t, kt + 1)
                    act.activation(xt[:, kt, 1:N + 1], banks[bank + kt % 2][:, :],
                                   ACT.Copy).then_inc(xt_copied, 1)

            def chunk(t):
                for kt in range(KT):
                    if kt == 0:
                        wait(act, unit_done, t, UNIT_AT[("w3", FT - 1)] + 1 - NU)
                    act.activation(xs[:, 0, kt, :], xt[:, kt, 1:N + 1], ACT.Copy).then_inc(xs_hi, 1)
                for n in range(12):
                    if n % KT == KT - 1:
                        evacuate(t, n // KT)
                    if n + MIX_AHEAD < 12:
                        mix_first(t, n + MIX_AHEAD)
                        mix_second(t, n + MIX_AHEAD)
                for j in range(FT):
                    f = hidf[j % HID_SLOTS]
                    wait_unit(act, t, ("w1", j))
                    wait(act, hid_lo, t, j + 1 - HID_SLOTS)
                    act.activation(f[:, :], banks[2 * (j % 2)][:, :], ACT.Tanh, scale=0.5)\
                        .then_inc(gate_tanh, 1)
                    if j in (FLIP_AT, FLIP_AT + 1) and not is_last(t):
                        copy_xt(t + 1, (0, 1) if j == FLIP_AT else (2, 3), 2 - 2 * (j % 2))
                    wait(act, hid_full, t, j + 1)
                    wait(act, unit_done, t, UNIT_AT[("w2", (j - HID_SLOTS) % FT)] + 1
                         - (NU if j < HID_SLOTS else 0))
                    act.activation(hid[j % HID_SLOTS][:, 0, :], f[:, :], ACT.Copy).then_inc(hid_hi, 1)
                    c, stage = divmod(j, 4)
                    if stage == 0:
                        for i, a in enumerate((0, 1, 4, 5)):
                            wait(act, exp_arg, t, 4 * c + i + 1)
                            act.activation(tmp[a][:, :], tmp[a][:, :], ACT.Exp).then_inc(wkv_exp, 1)
                    if stage == 3:
                        wait(act, att_full, t, c + 1)
                        wait(act, unit_done, t, UNIT_AT[("wo", (c - 2) % KT)] + 1 - (NU if c < 2 else 0))
                        act.activation(att[c % 2][:, 0, :], tmp[6][:, :], ACT.Copy).then_inc(att_hi, 1)
                if not is_last(t):
                    for n in range(MIX_AHEAD):
                        mix_first(t + 1, n)
                        mix_second(t + 1, n)

            act.wait_ge(const_loaded, 32)
            act.activation(tmp[0][:, 0:KT], vec[:, 3, :], ACT.Exp).then_inc(decay_made, 1)
            act.wait_ge(decay_made, 1)
            act.activation(decay[:, :], tmp[0][:, 0:KT], ACT.Copy, scale=-1.0).then_inc(decay_made, 1)
            act.wait_ge(const_made, 2)
            copy_xt(0, (0, 1), 2)
            copy_xt(0, (2, 3), 0)
            for n in range(MIX_AHEAD):
                mix_first(0, n)
                mix_second(0, n)
            over_chunks(act, chunk)

        @block.vector
        def _(dve):
            steps = [0, 0]

            def step(ins):
                steps[0] += 1
                ins.then_inc(vec_step, 1)
                return steps[0]

            def wait_step(base, k):
                dve.wait_ge(vec_step, base + k)

            def token_stats(t, tt):
                if tt == 0:
                    wait(dve, x_loaded, t, 16)
                return step(dve.bn_stats(stats[:, tt, :], xn[:, tt, :]))

            def token_mean_var(tt):
                return step(dve.bn_aggr(mean_var[:, tt, :], stats[:, tt, :]))

            def add_eps(base, ready):
                wait_step(base, ready)
                dve.tensor_scalar(var_eps[:, :], mean_var[:, :, 1], EPS, None, ALU.add).then_inc(var_ready, 1)

            def normalise(t, tt):
                wait(dve, rstd_ready, t, 1)
                dve.tensor_scalar(xn[:, tt, :], xn[:, tt, :], mean_var[:, tt, 0:1], rstd[:, tt:tt + 1],
                                  ALU.subtract, ALU.mult).then_inc(xn_ready, 1)

            def mix_item(t, n):
                q, kt = divmod(n, KT)
                f = mixf[n % MIX_AHEAD]
                wait(dve, mix_prev, t, n + 1)
                dve.scalar_tensor_tensor(f[:, :], xt[:, kt, 1:N + 1], vec[:, q, kt:kt + 1], f[:, :],
                                         ALU.mult, ALU.add).then_inc(mix_full, 1)

            def mix_rest(t, n):
                f, m = mixf[n % MIX_AHEAD], mix[n % MIX_AHEAD]
                wait(dve, mix_hi, t, n + 1)
                dve.tensor_tensor(m[:, 1, :], f[:, :], m[:, 0, :].bitcast(f32), ALU.subtract)\
                    .then_inc(mix_lo, 1)

            def mix_items(t, first, end):
                mix_item(t, first)
                for n in range(first + 1, end):
                    mix_item(t, n)
                    mix_rest(t, n - 1)
                mix_rest(t, end - 1)

            def shift(t):
                dve.tensor_scalar(xt[:, :, 0:1], xt[:, :, N:N + 1],
                                  keep[:, bass.ds(t, 1)], None, ALU.mult).then_inc(shift_ready, 1)

            def wkv(t, base, c, stage, at):
                k, v, th = (kvr[:, q, c, :] for q in range(3))
                before = [pab[:, i, 0:N] for i in range(3)]
                after = [pab[:, i, 1:N + 1] for i in range(3)]
                w, u = decay[:, c:c + 1], vec[:, 4, c:c + 1]
                if stage == 0:
                    if c == 0:
                        wait(dve, kvr_ready, t, 12)
                    step(dve.tensor_copy(pab[:, :, 0], carry[:, c, :]))
                    top = step(dve.tensor_tensor_scan(after[0], w.to_broadcast([P, N]), k,
                                                      carry[:, c, 0:1], ALU.add, ALU.max))
                    wait_step(base, top)
                    dve.scalar_tensor_tensor(tmp[0][:, :], before[0], w, after[0], ALU.add,
                                             ALU.subtract).then_inc(exp_arg, 1)
                    peak = step(dve.scalar_tensor_tensor(tmp[3][:, :], k, u, before[0], ALU.add, ALU.max))
                    dve.tensor_tensor(tmp[1][:, :], k, after[0], ALU.subtract).then_inc(exp_arg, 1)
                    wait_step(base, peak)
                    dve.tensor_tensor(tmp[4][:, :], before[0], tmp[3][:, :], ALU.subtract).then_inc(exp_arg, 1)
                    dve.scalar_tensor_tensor(tmp[5][:, :], k, u, tmp[3][:, :], ALU.add,
                                             ALU.subtract).then_inc(exp_arg, 1)
                elif stage == 1:
                    wait(dve, wkv_exp, t, 4 * c + 4)
                    ev = step(dve.tensor_tensor(tmp[2][:, :], tmp[1][:, :], v, ALU.mult))
                    at["den"] = step(dve.tensor_tensor_scan(after[2], tmp[0][:, :], tmp[1][:, :],
                                                            carry[:, c, 2:3], ALU.mult, ALU.add))
                    wait_step(base, ev)
                    at["num"] = step(dve.tensor_tensor_scan(after[1], tmp[0][:, :], tmp[2][:, :],
                                                            carry[:, c, 1:2], ALU.mult, ALU.add))
                    at["ev"] = step(dve.tensor_tensor(tmp[3][:, :], tmp[5][:, :], v, ALU.mult))
                elif stage == 2:
                    wait_step(base, at["ev"])
                    d = step(dve.tensor_tensor(tmp[2][:, :], tmp[4][:, :], before[2], ALU.mult))
                    n = step(dve.tensor_tensor(tmp[6][:, :], tmp[4][:, :], before[1], ALU.mult))
                    wait_step(base, d)
                    at["d"] = step(dve.tensor_tensor(tmp[2][:, :], tmp[2][:, :], tmp[5][:, :], ALU.add))
                    wait_step(base, n)
                    at["n"] = step(dve.tensor_tensor(tmp[6][:, :], tmp[6][:, :], tmp[3][:, :], ALU.add))
                else:
                    wait_step(base, at["n"])
                    r = step(dve.reciprocal(tmp[2][:, :], tmp[2][:, :]))
                    kept = step(dve.tensor_tensor(carry_kept[:, :], pab[:, :, N],
                                                  keep3[:, bass.ds(t * 3 + 3, 3)], ALU.mult))
                    wait_step(base, r)
                    y = step(dve.tensor_tensor(tmp[6][:, :], tmp[6][:, :], tmp[2][:, :], ALU.mult))
                    wait_step(base, kept)
                    step(dve.tensor_tensor(carry[:, c, :], carry_kept[:, :],
                                           reset3[:, bass.ds(t * 3 + 3, 3)], ALU.add))
                    wait_step(base, y)
                    dve.scalar_tensor_tensor(tmp[6][:, :], th, 1.0, tmp[6][:, :], ALU.add,
                                             ALU.mult).then_inc(att_full, 1)

            def att_rest(t, c):
                wait(dve, att_hi, t, c + 1)
                dve.tensor_tensor(att[c % 2][:, 1, :], tmp[6][:, :], att[c % 2][:, 0, :].bitcast(f32),
                                  ALU.subtract).then_inc(att_lo, 1)

            def chunk(t):
                steps[0] = 0
                base = t * STEPS + steps[1]
                at = {}
                if not (isinstance(t, int) and t == 0):
                    wait_step(base, 0)
                for kt in range(KT):
                    wait(dve, xs_hi, t, kt + 1)
                    dve.tensor_tensor(xs[:, 1, kt, :], xt[:, kt, 1:N + 1], xs[:, 0, kt, :].bitcast(f32),
                                      ALU.subtract).then_inc(xs_lo, 1)
                mix_items(t, MIX_AHEAD, 12)
                for j in range(FT):
                    f, h, b = hidf[j % HID_SLOTS], hid[j % HID_SLOTS], 2 * (j % 2)
                    wait(dve, gate_tanh, t, j + 1)
                    g = step(dve.scalar_tensor_tensor(f[:, :], f[:, :], 1.0, banks[b][:, :], ALU.add, ALU.mult))
                    wait_unit(dve, t, ("w3", j))
                    wait_step(base, g)
                    dve.tensor_tensor(f[:, :], f[:, :], banks[b + 1][:, :], ALU.mult).then_inc(hid_full, 1)
                    c, stage = divmod(j, 4)
                    if stage == 0 and c:
                        att_rest(t, c - 1)
                    wkv(t, base, c, stage, at)
                    if not is_last(t):
                        if 1 < j <= TT + 1:
                            at["mean_var"] = token_mean_var(j - 2)
                        if 1 <= j <= TT:
                            token_stats(t + 1, j - 1)
                        if j == TT + 2:
                            add_eps(base, at["mean_var"])
                        if TT + 3 <= j < 2 * TT + 3:
                            normalise(t + 1, j - TT - 3)
                        if j == 2 * TT + 3:
                            shift(t + 1)
                    wait(dve, hid_hi, t, j + 1)
                    dve.tensor_tensor(h[:, 1, :], f[:, :], h[:, 0, :].bitcast(f32), ALU.subtract)\
                        .then_inc(hid_lo, 1)
                att_rest(t, KT - 1)
                if not is_last(t):
                    mix_items(t + 1, 0, MIX_AHEAD)
                wait(dve, res_loaded, t, 16)
                for tt in range(TT):
                    if tt < TT - 1:
                        wait(dve, acc_tile, t, tt + 1)
                    else:
                        wait(dve, unit_done, t, NU)
                    dve.tensor_tensor(res[:, tt, :], res[:, tt, :], acc[tt][:, :], ALU.add)\
                        .then_inc(out_ready, 1)
                if not is_last(t):
                    assert steps[0] == STEPS, steps

            dve.memset(half[:, :], -0.5).then_inc(const_made, 1)
            for table, value in ((keep, 1.0), (keep3, 1.0), (reset3, 0.0), (carry, 0.0)):
                at0 = step(dve.memset(table[:], value))
            wait_step(0, at0)
            rows = CHUNKS_PER_ROW
            step(dve.memset(keep[:, 0:CHUNKS + 1:rows], 0.0))
            step(dve.memset(keep3[:, :].rearrange("p (s a) -> p s a", a=3)[:, 0:CHUNKS + 1:rows, :], 0.0))
            step(dve.memset(reset3[:, :].rearrange("p (s a) -> p s a", a=3)[:, 0:CHUNKS + 1:rows, 0], START))
            step(dve.memset(carry[:, :, 0], START))
            dve.wait_ge(const_loaded, 32)
            dve.tensor_scalar(one_less_mu[:, :, :], vec[:, 0:3, :], -1.0, 1.0, ALU.mult, ALU.add)\
                .then_inc(const_made, 1)
            dve.wait_ge(decay_made, 2)
            for tt in range(TT):
                wait_step(0, token_stats(0, tt))
                done = token_mean_var(tt)
            add_eps(0, done)
            for tt in range(TT):
                normalise(0, tt)
            dve.memset(xt[:, :, 0], 0.0).then_inc(shift_ready, 1)
            steps[1] = steps[0]
            mix_items(0, 0, MIX_AHEAD)
            over_chunks(dve, chunk)


def prepare_weights(nc, w_units, hadamard, split, resident, banks, acc):
    f32, f32r = mybir.dt.float32, mybir.dt.float32r
    ALU, ACT = mybir.AluOpType, mybir.ActivationFunctionType
    RAW, SPLIT = 6, 4
    plain = [u for u in UNITS if u[0] != "w2"]
    turn = plain + [("w2", j) for j in range(FT)]
    to_store = [u for u in turn if u not in RESIDENT_AT]
    all_banks = banks + acc

    with ExitStack() as ctx:
        def sb(name, shape, dt=f32):
            return ctx.enter_context(nc.sbuf_tensor(name, shape, dt))

        def sem(name):
            return ctx.enter_context(nc.semaphore(name))

        raw = [sb(f"raw{i}", [P, C]) for i in range(RAW)]
        out = [sb(f"split{i}", [P, 2, C], f32r) for i in range(SPLIT)]
        fly = [sb(f"fly{i}", [P, FT, C]) for i in range(2)]
        had = sb("had", [P, P])

        had_loaded = sem("had_loaded")
        w2_loaded = sem("w2_loaded")
        w2_psum = sem("w2_psum")
        w2_copied = sem("w2_copied")
        fly_step = sem("fly_step")
        raw_loaded = [sem(f"raw_loaded{i}") for i in range(RAW)]
        unit_hi = sem("unit_hi")
        unit_lo = sem("unit_lo")
        stored = [sem(f"stored{i}") for i in range(SPLIT)]

        def buffers(unit):
            if unit in RESIDENT_AT:
                return resident[RESIDENT_AT[unit]], None
            n = to_store.index(unit)
            return out[n % SPLIT], n

        block = ctx.enter_context(nc.Block())

        @block.sync
        def _(sp):
            def load(i):
                name, j = plain[i]
                sp.dma_start(raw[i % RAW][:, :], w_units[name][j]).then_inc(raw_loaded[i % RAW], 16)

            for i in range(RAW):
                load(i)
            sp.dma_start(had[:, :], hadamard).then_inc(had_loaded, 16)
            sp.dma_start(fly[0][:, :, :], w_units["w2"].rearrange("j p c -> p j c")).then_inc(w2_loaded, 16)
            for i, unit in enumerate(turn):
                sp.wait_ge(unit_lo, i + 1)
                buf, n = buffers(unit)
                if n is not None:
                    sp.dma_start(split[UNIT_AT[unit]].rearrange("p (a c) -> p a c", a=2), buf[:, :, :].bitcast(f32))\
                        .then_inc(stored[n % SPLIT], 16)
                if i + RAW < len(plain):
                    load(i + RAW)
            for i in range(SPLIT):
                sp.wait_ge(stored[i], 16 * len(to_store[i::SPLIT]))

        @block.tensor
        def _(pe):
            pe.wait_ge(had_loaded, 16)
            pe.wait_ge(w2_loaded, 16)
            for j in range(FT):
                if j >= len(all_banks):
                    pe.wait_ge(w2_copied, j + 1 - len(all_banks))
                pe.matmul(all_banks[j % len(all_banks)][:, :], had[:, :], fly[0][:, j, :],
                          start=True, stop=True).then_inc(w2_psum, 1)

        @block.scalar
        def _(act):
            def hi(i):
                unit = turn[i]
                buf, n = buffers(unit)
                if i < len(plain):
                    act.wait_ge(raw_loaded[i % RAW], 16 * (i // RAW + 1))
                    src = raw[i % RAW][:, :]
                else:
                    act.wait_ge(fly_step, 8)
                    src = fly[1][:, unit[1], :]
                if n is not None and n >= SPLIT:
                    act.wait_ge(stored[n % SPLIT], 16 * (n // SPLIT))
                act.activation(buf[:, 0, :], src, ACT.Copy, scale=0.5 if unit[0] == "wo" else 1.0)\
                    .then_inc(unit_hi, 1)

            for i in range(len(plain)):
                hi(i)
            for j in range(FT):
                act.wait_ge(w2_psum, j + 1)
                act.activation(fly[1][:, j, :], all_banks[j % len(all_banks)][:, :], ACT.Copy,
                               scale=0.5 / float(np.sqrt(H))).then_inc(w2_copied, 1)
            for i in range(len(plain), NU):
                hi(i)

        @block.vector
        def _(dve):
            def lo(i):
                unit = turn[i]
                buf, _ = buffers(unit)
                src = raw[i % RAW][:, :] if i < len(plain) else fly[1][:, unit[1], :]
                dve.wait_ge(unit_hi, i + 1)
                dve.scalar_tensor_tensor(buf[:, 1, :], src, 0.5 if unit[0] == "wo" else 1.0,
                                         buf[:, 0, :].bitcast(f32), ALU.mult, ALU.subtract).then_inc(unit_lo, 1)

            for i in range(len(plain)):
                lo(i)
            dve.wait_ge(w2_copied, FT)
            half, a = 1, 1
            for stage in range(4):
                src = fly[a][:, :, :].rearrange("p (g two h) c -> p g two (h c)", two=2, h=half)
                dst = fly[1 - a][:, :, :].rearrange("p (g two h) c -> p g two (h c)", two=2, h=half)
                if stage:
                    dve.wait_ge(fly_step, 2 * stage)
                dve.tensor_tensor(dst[:, :, 0, :], src[:, :, 0, :], src[:, :, 1, :], ALU.add).then_inc(fly_step, 1)
                dve.tensor_tensor(dst[:, :, 1, :], src[:, :, 0, :], src[:, :, 1, :], ALU.subtract)\
                    .then_inc(fly_step, 1)
                half, a = 2 * half, 1 - a
            for i in range(len(plain), NU):
                lo(i)


STEPS = 15 * KT + FT + 2 * TT


def _square_units(w):
    return np.ascontiguousarray(w.T).reshape(KT, P, C)


def _up_units(w):
    return np.ascontiguousarray(w.reshape(FT, P, KT, P).transpose(0, 3, 2, 1)).reshape(FT, P, KT * P)


def kernel(L0_attn_x, L0_attn_mu_r, L0_attn_mu_k, L0_attn_mu_v, L0_attn_wkv_w, L0_attn_wkv_u,
           L0_attn_Wr, L0_attn_Wk, L0_attn_Wv, L0_attn_Wo, L0_ffn_W1, L0_ffn_W2, L0_ffn_W3):
    import concourse.bacc as bacc
    from concourse.bass_utils import run_bass_kernel_spmd

    weights = {
        "k": _square_units(np.asarray(L0_attn_Wk)), "v": _square_units(np.asarray(L0_attn_Wv)),
        "r": _square_units(np.asarray(L0_attn_Wr)), "wo": _square_units(np.asarray(L0_attn_Wo)),
        "w1": _up_units(np.asarray(L0_ffn_W1)), "w3": _up_units(np.asarray(L0_ffn_W3)),
        "w2": np.ascontiguousarray(np.asarray(L0_ffn_W2).T).reshape(FT, P, C),
    }
    vectors = np.stack([np.asarray(v).reshape(KT, P).T for v in
                        (L0_attn_mu_k, L0_attn_mu_v, L0_attn_mu_r, L0_attn_wkv_w, L0_attn_wkv_u)], axis=1)
    hadamard = np.ones((1, 1), np.float32)
    while len(hadamard) < P:
        hadamard = np.block([[hadamard, hadamard], [hadamard, -hadamard]])
    arrays = {
        "x": np.ascontiguousarray(np.asarray(L0_attn_x).reshape(B * T, C)),
        "vectors": np.ascontiguousarray(vectors),
        "hadamard": np.ascontiguousarray(hadamard, np.float32),
        "identity": np.eye(P, dtype=np.float32),
    } | {f"units_{n}": w for n, w in weights.items()}

    nc = bacc.Bacc("TRN2", target_bir_lowering=False, num_devices=1)
    ap = {n: nc.dram_tensor(n, a.shape, mybir.dt.from_np(a.dtype), kind="ExternalInput").ap()
          for n, a in arrays.items()}
    out = nc.dram_tensor("out", (B * T, C), mybir.dt.float32, kind="ExternalOutput").ap()
    build(nc, ap["x"], {n: ap[f"units_{n}"] for n in weights}, ap["vectors"], ap["hadamard"],
          ap["identity"], out)
    r = run_bass_kernel_spmd(nc, [arrays], core_ids=[0])
    return r.results[0]["out"].reshape(B, T, C)
```

```python
from contextlib import ExitStack

import concourse.bass as bass
import numpy as np
from concourse import mybir

B, T, C, H = 4, 2048, 512, 2048
P = 128
N = 512
CHUNKS = B * T // N
CHUNKS_PER_ROW = T // N
KT = C // P
TT = N // P
FT = H // P
EPS = 1e-5
START = -1e38

LAG = 2
RING = 4
RAW = 4
MIX_AHEAD = 3
HID_SLOTS = 3
FLIP_AT = 12


def unit_order():
    order = [(q, kt) for q in ("k", "v", "r") for kt in range(KT)]
    for j in range(FT):
        order += [("w1", j), ("w3", j)]
        if j >= LAG:
            order.append(("w2", j - LAG))
        c, behind = divmod(j - 5, 4)
        if behind == 0 and c >= 0:
            order.append(("wo", c))
    return order + [("w2", FT - 2), ("wo", KT - 1), ("w2", FT - 1)]


UNITS = unit_order()
UNIT_AT = {u: n for n, u in enumerate(UNITS)}
NU = len(UNITS)
PLAIN = [u for u in UNITS if u[0] != "w2"]
PLAIN_AT = {u: m for m, u in enumerate(PLAIN)}
RESIDENT = PLAIN[1::4]
RESIDENT_AT = {u: n for n, u in enumerate(RESIDENT)}
EARLY = 5
STREAMED = [u for u in UNITS if u not in RESIDENT_AT]
STREAMED_AT = {u: n for n, u in enumerate(STREAMED)}
TURNS = len(STREAMED) // RING
assert len(STREAMED) % RING == 0


POOL_COLUMNS, DVE_COLUMNS = slice(0, 224), slice(224, C)


def split_in_step(j):
    return [m for m, u in enumerate(PLAIN) if m >= 14 and (
        u[1] == j + 1 if u[0] != "wo" else (4 * u[1] + 5 if u[1] < KT - 1 else FT) == j + 1)]


def w2_split_in_step(j):
    return range(FT * j // 3, FT * (j + 1) // 3) if j < 3 else ()


def of_slot(units, slot):
    return [u for u in units if u in STREAMED_AT and STREAMED_AT[u] % RING == slot]


def build(nc, x, w_units, vectors, hadamard, identity, out):
    f32, f32r = mybir.dt.float32, mybir.dt.float32r
    ALU, ACT = mybir.AluOpType, mybir.ActivationFunctionType

    split = nc.dram_tensor("split_units", [NU, P, 2 * C], f32, kind="Internal").ap()
    x_v = x.rearrange("(s t p) c -> s p t c", t=TT, p=P)
    out_v = out.rearrange("(s t p) c -> s p t c", t=TT, p=P)

    ctx = ExitStack()
    with ctx:
        def sb(name, shape, dt=f32, stack=ctx):
            return stack.enter_context(nc.sbuf_tensor(name, shape, dt))

        def sem(name):
            return ctx.enter_context(nc.semaphore(name))

        ident = sb("ident", [P, P])
        had = sb("had", [P, P])
        vec = sb("vec", [P, 5, KT])
        one_less_mu = sb("one_less_mu", [P, 3, KT])
        decay = sb("decay", [P, KT])
        exp_w = sb("exp_w", [P, KT])
        keep = sb("keep", [P, CHUNKS + 1])
        keep3 = sb("keep3", [P, 3 * (CHUNKS + 1)])
        reset3 = sb("reset3", [P, 3 * (CHUNKS + 1)])
        half = sb("half", [P, TT])
        carry = sb("carry", [P, KT, 3])
        carry_kept = sb("carry_kept", [P, 3])
        stats = sb("stats", [P, TT, 6])
        mean_var = sb("mean_var", [P, TT, 2])
        var_eps = sb("var_eps", [P, TT])
        rstd = sb("rstd", [P, TT])
        banks = [ctx.enter_context(nc.psum_tensor(f"bank{i}", [P, N], f32)) for i in range(4)]
        acc = [ctx.enter_context(nc.psum_tensor(f"acc{i}", [P, C], f32)) for i in range(TT)]

        xn = sb("xn", [P, TT, C])
        xt = sb("xt", [P, KT, N + 1])
        xs = sb("xs", [P, 2, KT, N], f32r)
        mixf = [sb(f"mixf{i}", [P, N]) for i in range(MIX_AHEAD)]
        mix = [sb(f"mix{i}", [P, 2, N], f32r) for i in range(MIX_AHEAD)]
        kvr = sb("kvr", [P, 3, KT, N])
        hidf = [sb(f"hidf{i}", [P, N]) for i in range(HID_SLOTS)]
        hid = [sb(f"hid{i}", [P, 2, N], f32r) for i in range(HID_SLOTS)]
        raw = [sb(f"raw{i}", [P, C]) for i in range(RAW)]
        ring = [sb(f"ring{i}", [P, 2, C], f32r) for i in range(RING)]
        resident = [sb(f"resident{i}", [P, 2, C], f32r) for i in range(EARLY)]
        with ExitStack() as early:
            fly = [sb(f"fly{i}", [P, FT, C], f32, early) for i in range(2)]
        att = [sb(f"att{i}", [P, 2, N], f32r) for i in range(2)]
        tmp = [sb(f"tmp{i}", [P, N]) for i in range(7)]
        pab = sb("pab", [P, 3, N + 1])
        res = sb("res", [P, TT, C])
        resident += [sb(f"resident{i}", [P, 2, C], f32r) for i in range(EARLY, len(RESIDENT))]

        per = {}

        def counted(name, n):
            s = sem(name)
            per[s.name] = n
            return s

        const_loaded = sem("const_loaded")
        const_made = sem("const_made")
        decay_made = sem("decay_made")
        w2_loaded = [sem(f"w2_loaded{i}") for i in range(4)]
        raw_loaded = [sem(f"raw_loaded{i}") for i in range(RAW)]
        w2_stored = [sem(f"w2_stored{i}") for i in range(2)]
        unit_stored = [sem(f"unit_stored{i}") for i in range(RING)]
        x_loaded = counted("x_loaded", 16)
        res_loaded = counted("res_loaded", 16)
        out_stored = counted("out_stored", 16)
        slot_loaded = [counted(f"slot_loaded{i}", 16 * TURNS) for i in range(RING)]
        w2_psum = sem("w2_psum")
        w2_copied = sem("w2_copied")
        fly_dve = sem("fly_dve")
        fly_pool = sem("fly_pool")
        w2_hi, w2_lo = sem("w2_hi"), sem("w2_lo")
        unit_hi, unit_lo = sem("unit_hi"), sem("unit_lo")
        unit_done = counted("unit_done", NU)
        rkv_bank = counted("rkv_bank", 9)
        xt_psum = counted("xt_psum", KT)
        acc_tile = counted("acc_tile", TT - 1)
        kvr_ready = counted("kvr_ready", 12)
        mix_prev = counted("mix_prev", 12)
        mix_hi = counted("mix_hi", 12)
        xs_hi = counted("xs_hi", KT)
        xt_copied = counted("xt_copied", KT)
        wkv_exp = counted("wkv_exp", 16)
        gate_tanh = counted("gate_tanh", FT)
        hid_hi = counted("hid_hi", FT)
        att_hi = counted("att_hi", KT)
        mix_full = counted("mix_full", 12)
        mix_lo = counted("mix_lo", 12)
        xs_lo = counted("xs_lo", KT)
        exp_arg = counted("exp_arg", 16)
        hid_full = counted("hid_full", FT)
        hid_lo = counted("hid_lo", FT)
        att_full = counted("att_full", KT)
        att_lo = counted("att_lo", KT)
        out_ready = counted("out_ready", TT)
        var_ready = counted("var_ready", 1)
        xn_ready = counted("xn_ready", TT)
        shift_ready = counted("shift_ready", 1)
        vec_step = sem("vec_step")
        rstd_ready = counted("rstd_ready", 1)

        def wait(eng, s, t, k):
            value = t * per[s.name] + k
            if not isinstance(value, int) or value > 0:
                eng.wait_ge(s, value)

        def wait_unit(eng, t, unit):
            wait(eng, unit_done, t, UNIT_AT[unit] + 1)

        def wait_item(eng, t, n):
            wait(eng, unit_done, t, n + 1 if n >= 0 else n + 13 - NU)

        block = ctx.enter_context(nc.Block())

        def over_chunks(eng, chunk):
            chunk(0)
            with eng.Fori(1, CHUNKS - 1) as t:
                chunk(t)
            chunk(CHUNKS - 1)

        def is_last(t):
            return isinstance(t, int) and t == CHUNKS - 1

        @block.sync
        def _(sp):
            def rows(a, t):
                return a[bass.ds(t * N, N), :].rearrange("(t p) c -> p t c", p=P)

            def load_x(t):
                wait(sp, xt_psum, t - 1, KT)
                sp.dma_start(xn[:, :, :], rows(x, t)).then_inc(x_loaded, 16)

            def load_residual(t):
                if isinstance(t, int) and t == 0:
                    sp.wait_ge(w2_lo, FT)
                wait(sp, out_stored, t - 1, 16)
                sp.dma_start(res[:, :, :], rows(x, t)).then_inc(res_loaded, 16)

            def store(t):
                wait(sp, out_ready, t, TT)
                sp.dma_start(rows(out, t), res[:, :, :]).then_inc(out_stored, 16)

            def load_unit(t, unit):
                n = STREAMED_AT[unit]
                wait(sp, unit_done, t, UNIT_AT[STREAMED[n - RING]] + 1 - (NU if n < RING else 0))
                sp.dma_start(ring[n % RING][:, :, :].bitcast(f32),
                             split[UNIT_AT[unit]].rearrange("p (a c) -> p a c", a=2))\
                    .then_inc(slot_loaded[n % RING], 16)

            def load_raw(m):
                if m >= RAW:
                    sp.wait_ge(unit_lo, m + 1 - RAW)
                name, i = PLAIN[m]
                sp.dma_start(raw[m % RAW][:, :], w_units[name][i]).then_inc(raw_loaded[m % RAW], 16)

            def store_w2(j):
                sp.wait_ge(w2_lo, j + 1)
                sp.dma_start(split[UNIT_AT["w2", j]].rearrange("p (a c) -> p a c", a=2),
                             att[j % 2][:, :, :].bitcast(f32)).then_inc(w2_stored[j % 2], 16)

            def first_chunk():
                for n, unit in enumerate(UNITS):
                    if unit[0] == "w1":
                        for j in w2_split_in_step(unit[1]):
                            store_w2(j)
                    if unit[0] == "w2":
                        i, j = STREAMED_AT[unit], unit[1]
                        sp.wait_ge(w2_stored[j % 2], 16 * (j // 2 + 1))
                        stored = of_slot([u for u in PLAIN if UNIT_AT[u] < n], i % RING)
                        sp.wait_ge(unit_stored[i % RING], 16 * len(stored))
                        load_unit(0, unit)
                        continue
                    m = PLAIN_AT[unit]
                    sp.wait_ge(unit_lo, m + 1)
                    if unit in STREAMED_AT:
                        sp.dma_start(split[n].rearrange("p (a c) -> p a c", a=2),
                                     ring[STREAMED_AT[unit] % RING][:, :, :].bitcast(f32))\
                            .then_inc(unit_stored[STREAMED_AT[unit] % RING], 16)
                    if m + RAW < len(PLAIN):
                        load_raw(m + RAW)
                    if unit == ("w1", 1):
                        load_x(1)
                    if unit == ("w1", 6):
                        load_residual(0)

            def chunk(t):
                for n, unit in enumerate(STREAMED):
                    load_unit(t, unit)
                    if n == 4 and not is_last(t):
                        load_x(t + 1)
                    if n == 9:
                        store(t - 1)
                    if n == 20:
                        load_residual(t)

            sp.dma_start(xn[:, :, :], rows(x, 0)).then_inc(x_loaded, 16)
            sp.dma_start(ident[:, :], identity).then_inc(const_loaded, 16)
            sp.dma_start(vec[:, :, :], vectors).then_inc(const_loaded, 16)
            for m in range(RAW):
                load_raw(m)
            sp.dma_start(had[:, :], hadamard).then_inc(const_loaded, 16)
            for i in range(4):
                sp.dma_start(fly[0][:, 4 * i:4 * i + 4, :],
                             w_units["w2"][4 * i:4 * i + 4].rearrange("j p c -> p j c")).then_inc(w2_loaded[i], 16)
            first_chunk()
            for i in range(RING):
                sp.wait_ge(unit_stored[i], 16 * len(of_slot(PLAIN, i)))
            with sp.Fori(1, CHUNKS - 1) as t:
                chunk(t)
            chunk(CHUNKS - 1)
            store(CHUNKS - 1)
            wait(sp, out_stored, CHUNKS - 1, 16)

        def butterflies(eng, done, half_stage, cols):
            stage, difference = divmod(half_stage, 2)
            h = 2 ** stage
            view = "p (g two h) c -> p g two h c"
            src, dst = (fly[(stage + i) % 2][:, :, :].rearrange(view, two=2, h=h) for i in (1, 0))
            if not stage:
                eng.wait_ge(w2_copied, FT)
            elif not difference:
                eng.wait_ge(done, 2 * stage)
            for g in range(FT // (2 * h)):
                last = eng.tensor_tensor(dst[:, g, difference, :, cols], src[:, g, 0, :, cols],
                                         src[:, g, 1, :, cols], ALU.subtract if difference else ALU.add)
            last.then_inc(done, 1)

        @block.gpsimd
        def _(pool):
            def inverse_root(t):
                wait(pool, var_ready, t, 1)
                pool.tensor_tensor(rstd[:, :], var_eps[:, :], half[:, :], ALU.pow).then_inc(rstd_ready, 1)

            pool.wait_ge(const_made, 1)
            inverse_root(0)
            for i in range(8):
                butterflies(pool, fly_pool, i, POOL_COLUMNS)
            inverse_root(1)
            with pool.Fori(2, CHUNKS) as t:
                inverse_root(t)

        @block.tensor
        def _(pe):
            def weights(t, unit):
                first = isinstance(t, int) and t == 0
                if first and unit in PLAIN_AT:
                    pe.wait_ge(unit_lo, PLAIN_AT[unit] + 1)
                if unit in RESIDENT_AT:
                    return resident[RESIDENT_AT[unit]]
                n = STREAMED_AT[unit]
                w2 = of_slot([("w2", j) for j in range(FT)], n % RING)
                if first and unit in w2:
                    pe.wait_ge(slot_loaded[n % RING], 16 * (w2.index(unit) + 1))
                elif not first:
                    wait(pe, slot_loaded[n % RING], t, 16 * (n // RING + 1 + len(w2) - TURNS))
                return ring[n % RING]

            def transposes(t, kts, into):
                wait(pe, xn_ready, t, TT)
                for kt in kts:
                    for tt in range(TT):
                        last = pe.transpose(banks[into + kt % 2][:, tt * P:(tt + 1) * P],
                                            xn[:, tt, kt * P:(kt + 1) * P], ident[:, :])
                    last.then_inc(xt_psum, 1)

            def rkv_item(t, n):
                q, kt = divmod(n, KT)
                w = weights(t, UNITS[n])
                m_in = mix[n % MIX_AHEAD]
                wait(pe, mix_hi, t, n + 1)
                wait(pe, mix_lo, t, n + 1)
                for m in range(KT):
                    if kt == 0:
                        if q == 0 and m % 2 == 0:
                            wait(pe, hid_full, t - 1, FT - 1 + m // 2)
                        elif q:
                            wait(pe, kvr_ready, t, KT * (q - 1) + m + 1)
                    col = slice(m * P, (m + 1) * P)
                    pe.matmul(banks[m][:, :], w[:, 0, col], m_in[:, 0, :], start=kt == 0, stop=False)
                    pe.matmul(banks[m][:, :], w[:, 1, col], m_in[:, 0, :], start=False, stop=False)
                    last = pe.matmul(banks[m][:, :], w[:, 0, col], m_in[:, 1, :], start=False,
                                     stop=kt == KT - 1)
                    if m == KT - 1:
                        last.then_inc(unit_done, 1)
                    elif kt == KT - 1:
                        last.then_inc(rkv_bank, 1)

            def up(t, j):
                b = 2 * (j % 2)
                if j == 0:
                    wait(pe, kvr_ready, t, 10)
                    wait(pe, xs_hi, t, KT)
                    wait(pe, xs_lo, t, KT)
                elif j == 1:
                    wait(pe, kvr_ready, t, 12)
                else:
                    wait(pe, hid_full, t, j - 1)
                if j in (FLIP_AT + 1, FLIP_AT + 2) and not is_last(t):
                    wait(pe, xt_copied, t + 1, 2 * (j - FLIP_AT))
                for n, name in enumerate(("w1", "w3")):
                    w = weights(t, (name, j))
                    for kt in range(KT):
                        col = slice(kt * P, (kt + 1) * P)
                        pe.matmul(banks[b + n][:, :], w[:, 0, col], xs[:, 0, kt, :], start=kt == 0, stop=False)
                        pe.matmul(banks[b + n][:, :], w[:, 1, col], xs[:, 0, kt, :], start=False, stop=False)
                        last = pe.matmul(banks[b + n][:, :], w[:, 0, col], xs[:, 1, kt, :], start=False,
                                         stop=kt == KT - 1)
                    last.then_inc(unit_done, 1)

            def down(t, unit, a, first=False, final=False):
                w = weights(t, unit)
                for tt in range(TT):
                    col = slice(tt * P, (tt + 1) * P)
                    if first:
                        wait(pe, out_ready, t - 1, tt + 1)
                    pe.matmul(acc[tt][:, :], a[:, 0, col], w[:, 0, :], start=first, stop=False)
                    pe.matmul(acc[tt][:, :], a[:, 1, col], w[:, 0, :], start=False, stop=False)
                    last = pe.matmul(acc[tt][:, :], a[:, 0, col], w[:, 1, :], start=False, stop=final)
                    if tt == TT - 1:
                        last.then_inc(unit_done, 1)
                    elif final:
                        last.then_inc(acc_tile, 1)

            def ffn_down(t, j):
                wait(pe, hid_hi, t, j + 1)
                wait(pe, hid_lo, t, j + 1)
                down(t, ("w2", j), hid[j % HID_SLOTS], first=j == 0, final=j == FT - 1)

            def att_down(t, c):
                wait(pe, att_hi, t, c + 1)
                wait(pe, att_lo, t, c + 1)
                down(t, ("wo", c), att[c % 2])

            def chunk(t):
                for n in range(12):
                    rkv_item(t, n)
                for j in range(FT):
                    up(t, j)
                    if j in (FLIP_AT, FLIP_AT + 1) and not is_last(t):
                        wait(pe, hid_full, t, j)
                        transposes(t + 1, (0, 1) if j == FLIP_AT else (2, 3), 2 - 2 * (j % 2))
                    if j >= LAG:
                        ffn_down(t, j - LAG)
                    if j >= 5 and j % 4 == 1:
                        att_down(t, (j - 5) // 4)
                ffn_down(t, FT - 2)
                att_down(t, KT - 1)
                ffn_down(t, FT - 1)

            pe.wait_ge(const_loaded, 48)
            transposes(0, (0, 1), 2)
            transposes(0, (2, 3), 0)
            for j in range(FT):
                pe.wait_ge(w2_loaded[j // 4], 16)
                if j >= TT:
                    pe.wait_ge(w2_copied, j + 1 - TT)
                pe.matmul(acc[j % TT][:, :], had[:, :], fly[0][:, j, :], start=True, stop=True).then_inc(w2_psum, 1)
            over_chunks(pe, chunk)

        @block.scalar
        def _(act):
            def mix_first(t, n):
                q, kt = divmod(n, KT)
                if n == 0:
                    wait(act, xt_copied, t, KT)
                    wait(act, shift_ready, t, 1)
                wait(act, mix_lo, t, n + 1 - MIX_AHEAD)
                act.activation(mixf[n % MIX_AHEAD][:, :], xt[:, kt, 0:N], ACT.Copy,
                               scale=one_less_mu[:, q, kt:kt + 1]).then_inc(mix_prev, 1)

            def mix_second(t, n):
                wait(act, mix_full, t, n + 1)
                wait_item(act, t, n - MIX_AHEAD)
                act.activation(mix[n % MIX_AHEAD][:, 0, :], mixf[n % MIX_AHEAD][:, :],
                               ACT.Copy).then_inc(mix_hi, 1)

            def evacuate(t, q):
                for m in range(KT):
                    if m < KT - 1:
                        wait(act, rkv_bank, t, 3 * q + m + 1)
                    else:
                        wait_item(act, t, 4 * q + 3)
                    if q == 0 and m == 0:
                        wait(act, att_full, t - 1, KT)
                    act.activation(kvr[:, q, m, :], banks[m][:, :], ACT.Tanh if q == 2 else ACT.Copy,
                                   scale=0.5 if q == 2 else 1.0).then_inc(kvr_ready, 1)

            def copy_xt(t, kts, bank):
                wait(act, shift_ready, t, 1)
                for kt in kts:
                    wait(act, xt_psum, t, kt + 1)
                    act.activation(xt[:, kt, 1:N + 1], banks[bank + kt % 2][:, :],
                                   ACT.Copy).then_inc(xt_copied, 1)

            def split_hi(m):
                unit = PLAIN[m]
                act.wait_ge(raw_loaded[m % RAW], 16 * (m // RAW + 1))
                if unit in RESIDENT_AT:
                    dst = resident[RESIDENT_AT[unit]]
                    if RESIDENT_AT[unit] == EARLY:
                        act.wait_ge(w2_lo, FT)
                else:
                    n = STREAMED_AT[unit]
                    dst = ring[n % RING]
                    if n >= RING:
                        act.wait_ge(unit_done, UNIT_AT[STREAMED[n - RING]] + 1)
                        stored = of_slot([u for u in PLAIN[:m]], n % RING)
                        act.wait_ge(unit_stored[n % RING], 16 * len(stored))
                act.activation(dst[:, 0, :], raw[m % RAW][:, :], ACT.Copy,
                               scale=0.5 if unit[0] == "wo" else 1.0).then_inc(unit_hi, 1)

            def split_w2_hi(j):
                if j == 0:
                    act.wait_ge(fly_dve, 8)
                    act.wait_ge(fly_pool, 8)
                if j >= 2:
                    act.wait_ge(w2_stored[j % 2], 16 * (j // 2))
                act.activation(att[j % 2][:, 0, :], fly[1][:, j, :], ACT.Copy).then_inc(w2_hi, 1)

            def exponentials(t, c):
                for i, a in enumerate((0, 1, 4, 5)):
                    wait(act, exp_arg, t, 4 * c + i + 1)
                    act.activation(tmp[a][:, :], tmp[a][:, :], ACT.Exp).then_inc(wkv_exp, 1)

            def chunk(t):
                first = isinstance(t, int) and t == 0
                wait(act, unit_done, t, UNIT_AT[("w3", FT - 1)] + 1 - NU)
                for kt in range(KT):
                    act.activation(xs[:, 0, kt, :], xt[:, kt, 1:N + 1], ACT.Copy).then_inc(xs_hi, 1)
                mix_first(t, MIX_AHEAD)
                for n in range(12):
                    if n % KT == KT - 1:
                        evacuate(t, n // KT)
                    if n + MIX_AHEAD < 12:
                        mix_second(t, n + MIX_AHEAD)
                    if n + MIX_AHEAD + 1 < 12:
                        mix_first(t, n + MIX_AHEAD + 1)
                    if first and n + RAW < 14:
                        split_hi(n + RAW)
                exponentials(t, 0)
                for j in range(FT):
                    f = hidf[j % HID_SLOTS]
                    wait_unit(act, t, ("w1", j))
                    wait(act, hid_lo, t, j + 1 - HID_SLOTS)
                    act.activation(f[:, :], banks[2 * (j % 2)][:, :], ACT.Tanh, scale=0.5)\
                        .then_inc(gate_tanh, 1)
                    if j in (FLIP_AT, FLIP_AT + 1) and not is_last(t):
                        copy_xt(t + 1, (0, 1) if j == FLIP_AT else (2, 3), 2 - 2 * (j % 2))
                    wait(act, hid_full, t, j + 1)
                    wait(act, unit_done, t, UNIT_AT[("w2", (j - HID_SLOTS) % FT)] + 1
                         - (NU if j < HID_SLOTS else 0))
                    act.activation(hid[j % HID_SLOTS][:, 0, :], f[:, :], ACT.Copy).then_inc(hid_hi, 1)
                    if first:
                        for m in split_in_step(j):
                            split_hi(m)
                        for i in w2_split_in_step(j):
                            split_w2_hi(i)
                    c, stage = divmod(j + 1, 4)
                    if stage == 0 and c < KT:
                        exponentials(t, c)
                    if stage == 3:
                        wait(act, att_full, t, c + 1)
                        if first and c < 2:
                            act.wait_ge(w2_stored[c], 8 * FT)
                        wait(act, unit_done, t, UNIT_AT[("wo", (c - 2) % KT)] + 1 - (NU if c < 2 else 0))
                        act.activation(att[c % 2][:, 0, :], tmp[6][:, :], ACT.Copy).then_inc(att_hi, 1)
                if not is_last(t):
                    mix_first(t + 1, 0)
                    for n in range(MIX_AHEAD):
                        if n + 1 < MIX_AHEAD:
                            mix_first(t + 1, n + 1)
                        mix_second(t + 1, n)

            act.wait_ge(const_loaded, 48)
            act.activation(exp_w[:, :], vec[:, 3, :], ACT.Exp).then_inc(decay_made, 1)
            act.wait_ge(decay_made, 1)
            act.activation(decay[:, :], exp_w[:, :], ACT.Copy, scale=-1.0).then_inc(decay_made, 1)
            for m in range(2):
                split_hi(m)
            act.wait_ge(const_made, 2)
            copy_xt(0, (0, 1), 2)
            copy_xt(0, (2, 3), 0)
            mix_first(0, 0)
            for n in range(MIX_AHEAD):
                if n + 1 < MIX_AHEAD:
                    mix_first(0, n + 1)
                mix_second(0, n)
            for m in range(2, RAW):
                split_hi(m)
            for j in range(FT):
                act.wait_ge(w2_psum, j + 1)
                act.activation(fly[1][:, j, :], acc[j % TT][:, :], ACT.Copy,
                               scale=0.5 / float(np.sqrt(H))).then_inc(w2_copied, 1)
            over_chunks(act, chunk)

        @block.vector
        def _(dve):
            steps = [0, 0]

            def step(ins):
                steps[0] += 1
                ins.then_inc(vec_step, 1)
                return steps[0]

            def wait_step(base, k):
                dve.wait_ge(vec_step, base + k)

            def token_stats(t, tt):
                if tt == 0:
                    wait(dve, x_loaded, t, 16)
                return step(dve.bn_stats(stats[:, tt, :], xn[:, tt, :]))

            def token_mean_var(tt):
                return step(dve.bn_aggr(mean_var[:, tt, :], stats[:, tt, :]))

            def add_eps(base, ready):
                wait_step(base, ready)
                dve.tensor_scalar(var_eps[:, :], mean_var[:, :, 1], EPS, None, ALU.add).then_inc(var_ready, 1)

            def normalise(t, tt):
                wait(dve, rstd_ready, t, 1)
                dve.tensor_scalar(xn[:, tt, :], xn[:, tt, :], mean_var[:, tt, 0:1], rstd[:, tt:tt + 1],
                                  ALU.subtract, ALU.mult).then_inc(xn_ready, 1)

            def mix_item(t, n):
                q, kt = divmod(n, KT)
                f = mixf[n % MIX_AHEAD]
                wait(dve, mix_prev, t, n + 1)
                dve.scalar_tensor_tensor(f[:, :], xt[:, kt, 1:N + 1], vec[:, q, kt:kt + 1], f[:, :],
                                         ALU.mult, ALU.add).then_inc(mix_full, 1)

            def mix_rest(t, n):
                f, m = mixf[n % MIX_AHEAD], mix[n % MIX_AHEAD]
                wait(dve, mix_hi, t, n + 1)
                dve.tensor_tensor(m[:, 1, :], f[:, :], m[:, 0, :].bitcast(f32), ALU.subtract)\
                    .then_inc(mix_lo, 1)

            def mix_items(t, first, end):
                mix_item(t, first)
                for n in range(first + 1, end):
                    mix_item(t, n)
                    mix_rest(t, n - 1)
                mix_rest(t, end - 1)

            def shift(t):
                dve.tensor_scalar(xt[:, :, 0:1], xt[:, :, N:N + 1],
                                  keep[:, bass.ds(t, 1)], None, ALU.mult).then_inc(shift_ready, 1)

            def wkv(t, base, c, stage, at):
                k, v, th = (kvr[:, q, c, :] for q in range(3))
                before = [pab[:, i, 0:N] for i in range(3)]
                after = [pab[:, i, 1:N + 1] for i in range(3)]
                w, u = decay[:, c:c + 1], vec[:, 4, c:c + 1]
                if stage == 0:
                    if c == 0:
                        wait(dve, kvr_ready, t, 12)
                    step(dve.tensor_copy(pab[:, :, 0], carry[:, c, :]))
                    top = step(dve.tensor_tensor_scan(after[0], w.to_broadcast([P, N]), k,
                                                      carry[:, c, 0:1], ALU.add, ALU.max))
                    wait_step(base, top)
                    dve.scalar_tensor_tensor(tmp[0][:, :], before[0], w, after[0], ALU.add,
                                             ALU.subtract).then_inc(exp_arg, 1)
                    peak = step(dve.scalar_tensor_tensor(tmp[3][:, :], k, u, before[0], ALU.add, ALU.max))
                    dve.tensor_tensor(tmp[1][:, :], k, after[0], ALU.subtract).then_inc(exp_arg, 1)
                    wait_step(base, peak)
                    dve.tensor_tensor(tmp[4][:, :], before[0], tmp[3][:, :], ALU.subtract).then_inc(exp_arg, 1)
                    dve.scalar_tensor_tensor(tmp[5][:, :], k, u, tmp[3][:, :], ALU.add,
                                             ALU.subtract).then_inc(exp_arg, 1)
                elif stage == 1:
                    wait(dve, wkv_exp, t, 4 * c + 4)
                    ev = step(dve.tensor_tensor(tmp[2][:, :], tmp[1][:, :], v, ALU.mult))
                    at["den"] = step(dve.tensor_tensor_scan(after[2], tmp[0][:, :], tmp[1][:, :],
                                                            carry[:, c, 2:3], ALU.mult, ALU.add))
                    wait_step(base, ev)
                    at["num"] = step(dve.tensor_tensor_scan(after[1], tmp[0][:, :], tmp[2][:, :],
                                                            carry[:, c, 1:2], ALU.mult, ALU.add))
                    at["ev"] = step(dve.tensor_tensor(tmp[3][:, :], tmp[5][:, :], v, ALU.mult))
                elif stage == 2:
                    wait_step(base, at["ev"])
                    d = step(dve.tensor_tensor(tmp[2][:, :], tmp[4][:, :], before[2], ALU.mult))
                    n = step(dve.tensor_tensor(tmp[6][:, :], tmp[4][:, :], before[1], ALU.mult))
                    wait_step(base, d)
                    at["d"] = step(dve.tensor_tensor(tmp[2][:, :], tmp[2][:, :], tmp[5][:, :], ALU.add))
                    wait_step(base, n)
                    at["n"] = step(dve.tensor_tensor(tmp[6][:, :], tmp[6][:, :], tmp[3][:, :], ALU.add))
                else:
                    wait_step(base, at["n"])
                    r = step(dve.reciprocal(tmp[2][:, :], tmp[2][:, :]))
                    kept = step(dve.tensor_tensor(carry_kept[:, :], pab[:, :, N],
                                                  keep3[:, bass.ds(t * 3 + 3, 3)], ALU.mult))
                    wait_step(base, r)
                    y = step(dve.tensor_tensor(tmp[6][:, :], tmp[6][:, :], tmp[2][:, :], ALU.mult))
                    wait_step(base, kept)
                    step(dve.tensor_tensor(carry[:, c, :], carry_kept[:, :],
                                           reset3[:, bass.ds(t * 3 + 3, 3)], ALU.add))
                    wait_step(base, y)
                    dve.scalar_tensor_tensor(tmp[6][:, :], th, 1.0, tmp[6][:, :], ALU.add,
                                             ALU.mult).then_inc(att_full, 1)

            def att_rest(t, c):
                wait(dve, att_hi, t, c + 1)
                dve.tensor_tensor(att[c % 2][:, 1, :], tmp[6][:, :], att[c % 2][:, 0, :].bitcast(f32),
                                  ALU.subtract).then_inc(att_lo, 1)

            def split_lo(m):
                unit = PLAIN[m]
                dst = resident[RESIDENT_AT[unit]] if unit in RESIDENT_AT else ring[STREAMED_AT[unit] % RING]
                dve.wait_ge(unit_hi, m + 1)
                dve.scalar_tensor_tensor(dst[:, 1, :], raw[m % RAW][:, :], 0.5 if unit[0] == "wo" else 1.0,
                                         dst[:, 0, :].bitcast(f32), ALU.mult, ALU.subtract).then_inc(unit_lo, 1)

            def split_w2_lo(j):
                dve.wait_ge(w2_hi, j + 1)
                dve.tensor_tensor(att[j % 2][:, 1, :], fly[1][:, j, :], att[j % 2][:, 0, :].bitcast(f32),
                                  ALU.subtract).then_inc(w2_lo, 1)

            def chunk(t):
                steps[0] = 0
                first = isinstance(t, int) and t == 0
                base = t * STEPS + steps[1]
                at = {}
                if not first:
                    wait_step(base, 0)
                mix_item(t, MIX_AHEAD)
                for n in range(MIX_AHEAD, 12):
                    if n + 1 < 12:
                        mix_item(t, n + 1)
                    mix_rest(t, n)
                    if n == 7:
                        for kt in range(KT):
                            wait(dve, xs_hi, t, kt + 1)
                            dve.tensor_tensor(xs[:, 1, kt, :], xt[:, kt, 1:N + 1],
                                              xs[:, 0, kt, :].bitcast(f32), ALU.subtract).then_inc(xs_lo, 1)
                    if first:
                        split_lo(n + RAW - MIX_AHEAD)
                        if n >= 4:
                            butterflies(dve, fly_dve, n - 4, DVE_COLUMNS)
                if first:
                    split_lo(13)
                    dve.wait_ge(fly_pool, 8)
                    dve.wait_ge(fly_dve, 8)
                wkv(t, base, 0, 0, at)
                for j in range(FT):
                    f, h, b = hidf[j % HID_SLOTS], hid[j % HID_SLOTS], 2 * (j % 2)
                    wait(dve, gate_tanh, t, j + 1)
                    g = step(dve.scalar_tensor_tensor(f[:, :], f[:, :], 1.0, banks[b][:, :], ALU.add, ALU.mult))
                    wait_unit(dve, t, ("w3", j))
                    wait_step(base, g)
                    dve.tensor_tensor(f[:, :], f[:, :], banks[b + 1][:, :], ALU.mult).then_inc(hid_full, 1)
                    if first:
                        for m in split_in_step(j):
                            split_lo(m)
                        for i in w2_split_in_step(j):
                            split_w2_lo(i)
                    c, stage = divmod(j + 1, 4)
                    if stage == 0:
                        att_rest(t, c - 1)
                    if c < KT:
                        wkv(t, base, c, stage, at)
                    if not is_last(t):
                        if 1 < j <= TT + 1:
                            at["mean_var"] = token_mean_var(j - 2)
                        if 1 <= j <= TT:
                            token_stats(t + 1, j - 1)
                        if j == TT + 2:
                            add_eps(base, at["mean_var"])
                        if TT + 3 <= j < 2 * TT + 3:
                            normalise(t + 1, j - TT - 3)
                        if j == 2 * TT + 3:
                            shift(t + 1)
                    wait(dve, hid_hi, t, j + 1)
                    dve.tensor_tensor(h[:, 1, :], f[:, :], h[:, 0, :].bitcast(f32), ALU.subtract)\
                        .then_inc(hid_lo, 1)
                if not is_last(t):
                    mix_items(t + 1, 0, MIX_AHEAD)
                wait(dve, res_loaded, t, 16)
                for tt in range(TT):
                    if tt < TT - 1:
                        wait(dve, acc_tile, t, tt + 1)
                    else:
                        wait(dve, unit_done, t, NU)
                    dve.tensor_tensor(res[:, tt, :], res[:, tt, :], acc[tt][:, :], ALU.add)\
                        .then_inc(out_ready, 1)
                if not is_last(t):
                    assert steps[0] == STEPS, steps

            dve.memset(half[:, :], -0.5).then_inc(const_made, 1)
            for table, value in ((keep, 1.0), (keep3, 1.0), (reset3, 0.0), (carry, 0.0)):
                at0 = step(dve.memset(table[:], value))
            wait_step(0, at0)
            rows = CHUNKS_PER_ROW
            step(dve.memset(keep[:, 0:CHUNKS + 1:rows], 0.0))
            step(dve.memset(keep3[:, :].rearrange("p (s a) -> p s a", a=3)[:, 0:CHUNKS + 1:rows, :], 0.0))
            step(dve.memset(reset3[:, :].rearrange("p (s a) -> p s a", a=3)[:, 0:CHUNKS + 1:rows, 0], START))
            step(dve.memset(carry[:, :, 0], START))
            dve.wait_ge(const_loaded, 48)
            dve.tensor_scalar(one_less_mu[:, :, :], vec[:, 0:3, :], -1.0, 1.0, ALU.mult, ALU.add)\
                .then_inc(const_made, 1)
            dve.wait_ge(decay_made, 2)
            for tt in range(TT):
                wait_step(0, token_stats(0, tt))
                done = token_mean_var(tt)
            add_eps(0, done)
            for tt in range(TT):
                normalise(0, tt)
            dve.memset(xt[:, :, 0], 0.0).then_inc(shift_ready, 1)
            steps[1] = steps[0]
            for m in range(2):
                split_lo(m)
            mix_items(0, 0, MIX_AHEAD)
            for m in range(2, RAW):
                split_lo(m)
            over_chunks(dve, chunk)


STEPS = 15 * KT + FT + 2 * TT


def _square_units(w):
    return np.ascontiguousarray(w.T).reshape(KT, P, C)


def _up_units(w):
    return np.ascontiguousarray(w.reshape(FT, P, KT, P).transpose(0, 3, 2, 1)).reshape(FT, P, KT * P)


def kernel(L0_attn_x, L0_attn_mu_r, L0_attn_mu_k, L0_attn_mu_v, L0_attn_wkv_w, L0_attn_wkv_u,
           L0_attn_Wr, L0_attn_Wk, L0_attn_Wv, L0_attn_Wo, L0_ffn_W1, L0_ffn_W2, L0_ffn_W3):
    import concourse.bacc as bacc
    from concourse.bass_utils import run_bass_kernel_spmd

    weights = {
        "k": _square_units(np.asarray(L0_attn_Wk)), "v": _square_units(np.asarray(L0_attn_Wv)),
        "r": _square_units(np.asarray(L0_attn_Wr)), "wo": _square_units(np.asarray(L0_attn_Wo)),
        "w1": _up_units(np.asarray(L0_ffn_W1)), "w3": _up_units(np.asarray(L0_ffn_W3)),
        "w2": np.ascontiguousarray(np.asarray(L0_ffn_W2).T).reshape(FT, P, C),
    }
    vectors = np.stack([np.asarray(v).reshape(KT, P).T for v in
                        (L0_attn_mu_k, L0_attn_mu_v, L0_attn_mu_r, L0_attn_wkv_w, L0_attn_wkv_u)], axis=1)
    hadamard = np.ones((1, 1), np.float32)
    while len(hadamard) < P:
        hadamard = np.block([[hadamard, hadamard], [hadamard, -hadamard]])
    arrays = {
        "x": np.ascontiguousarray(np.asarray(L0_attn_x).reshape(B * T, C)),
        "vectors": np.ascontiguousarray(vectors),
        "hadamard": np.ascontiguousarray(hadamard, np.float32),
        "identity": np.eye(P, dtype=np.float32),
    } | {f"units_{n}": w for n, w in weights.items()}

    nc = bacc.Bacc("TRN2", target_bir_lowering=False, num_devices=1)
    ap = {n: nc.dram_tensor(n, a.shape, mybir.dt.from_np(a.dtype), kind="ExternalInput").ap()
          for n, a in arrays.items()}
    out = nc.dram_tensor("out", (B * T, C), mybir.dt.float32, kind="ExternalOutput").ap()
    build(nc, ap["x"], {n: ap[f"units_{n}"] for n in weights}, ap["vectors"], ap["hadamard"],
          ap["identity"], out)
    r = run_bass_kernel_spmd(nc, [arrays], core_ids=[0])
    return r.results[0]["out"].reshape(B, T, C)
```

```python
from contextlib import ExitStack

import concourse.bass as bass
import numpy as np
from concourse import mybir

B, T, C, H = 4, 2048, 512, 2048
P = 128
N = 512
CHUNKS = B * T // N
CHUNKS_PER_ROW = T // N
KT = C // P
TT = N // P
FT = H // P
EPS = 1e-5
START = -1e38

LAG = 2
RING = 4
W2_LOADS = 4
RAW = 4
MIX_AHEAD = 3
HID_SLOTS = 3
FLIP_AT = 12


def unit_order():
    order = [(q, kt) for q in ("k", "v", "r") for kt in range(KT)]
    for j in range(FT):
        order += [("w1", j), ("w3", j)]
        if j >= LAG:
            order.append(("w2", j - LAG))
        c, behind = divmod(j - 5, 4)
        if behind == 0 and c >= 0:
            order.append(("wo", c))
    return order + [("w2", FT - 2), ("wo", KT - 1), ("w2", FT - 1)]


UNITS = unit_order()
UNIT_AT = {u: n for n, u in enumerate(UNITS)}
NU = len(UNITS)
RESIDENT = [u for u in UNITS if u[0] != "w2"][1::4]
RESIDENT_AT = {u: n for n, u in enumerate(RESIDENT)}
EARLY = RESIDENT[:4]
STREAMED = [u for u in UNITS if u not in RESIDENT_AT]
STREAMED_AT = {u: n for n, u in enumerate(STREAMED)}
TURNS = len(STREAMED) // RING
assert len(STREAMED) % RING == 0

SPLIT_AHEAD = 4
LO_BY_DVE = 14
BY_DVE, BY_POOL = UNITS[:LO_BY_DVE], UNITS[LO_BY_DVE:]
RAW_ORDER = [u for u in UNITS if u[0] != "w2"]
POOL_COLUMNS, DVE_COLUMNS = slice(0, 288), slice(288, C)


def in_slot(units, slot):
    return [u for u in units if u not in EARLY and UNIT_AT[u] % RING == slot]


def split_in_step(j):
    units = units_of_step(j + 1) if j else []
    soon = [u for u in units if UNIT_AT[u] - RING <= UNIT_AT[("w1", j)]]
    return soon, units[len(soon):]


def units_of_step(j):
    return [u for u in UNITS[12:] if (
        j == (u[1] if u[0] in ("w1", "w3") else min(u[1] + LAG, FT) if u[0] == "w2"
              else min(4 * u[1] + 5, FT)))]


def build(nc, x, w_units, vectors, hadamard, identity, out):
    f32, f32r = mybir.dt.float32, mybir.dt.float32r
    ALU, ACT = mybir.AluOpType, mybir.ActivationFunctionType

    split = nc.dram_tensor("split_units", [NU, P, 2 * C], f32, kind="Internal").ap()

    ctx = ExitStack()
    with ctx:
        def sb(name, shape, dt=f32, stack=ctx):
            return stack.enter_context(nc.sbuf_tensor(name, shape, dt))

        def sem(name):
            return ctx.enter_context(nc.semaphore(name))

        ident = sb("ident", [P, P])
        had = sb("had", [P, P])
        vec = sb("vec", [P, 5, KT])
        one_less_mu = sb("one_less_mu", [P, 3, KT])
        decay = sb("decay", [P, KT])
        exp_w = sb("exp_w", [P, KT])
        keep = sb("keep", [P, CHUNKS + 1])
        keep3 = sb("keep3", [P, 3 * (CHUNKS + 1)])
        reset3 = sb("reset3", [P, 3 * (CHUNKS + 1)])
        half = sb("half", [P, TT])
        carry = sb("carry", [P, KT, 3])
        carry_kept = sb("carry_kept", [P, 3])
        stats = sb("stats", [P, TT, 6])
        mean_var = sb("mean_var", [P, TT, 2])
        var_eps = sb("var_eps", [P, TT])
        rstd = sb("rstd", [P, TT])
        banks = [ctx.enter_context(nc.psum_tensor(f"bank{i}", [P, N], f32)) for i in range(4)]
        acc = [ctx.enter_context(nc.psum_tensor(f"acc{i}", [P, C], f32)) for i in range(TT)]

        xn = sb("xn", [P, TT, C])
        xt = sb("xt", [P, KT, N + 1])
        xs = sb("xs", [P, 2, KT, N], f32r)
        mixf = [sb(f"mixf{i}", [P, N]) for i in range(MIX_AHEAD)]
        mix = [sb(f"mix{i}", [P, 2, N], f32r) for i in range(MIX_AHEAD)]
        kvr = sb("kvr", [P, 3, KT, N])
        hidf = [sb(f"hidf{i}", [P, N]) for i in range(HID_SLOTS - 1)]
        hid = [sb(f"hid{i}", [P, 2, N], f32r) for i in range(HID_SLOTS)]
        raw = [sb(f"raw{i}", [P, C]) for i in range(RAW)]
        ring = [sb(f"ring{i}", [P, 2, C], f32r) for i in range(RING)]
        res = sb("res", [P, TT, C])
        resident = [sb(f"resident{i}", [P, 2, C], f32r) for i in range(len(EARLY))]
        with ExitStack() as early:
            fly = [sb(f"fly{i}", [P, FT, C], f32, early) for i in range(2)]
        att = [sb(f"att{i}", [P, 2, N], f32r) for i in range(2)]
        tmp = [sb(f"tmp{i}", [P, N]) for i in range(7)]
        pab = sb("pab", [P, 3, N + 1])
        hidf.append(sb(f"hidf{HID_SLOTS - 1}", [P, N]))
        resident += [sb(f"resident{i}", [P, 2, C], f32r) for i in range(len(EARLY), len(RESIDENT))]

        per = {}

        def counted(name, n):
            s = sem(name)
            per[s.name] = n
            return s

        ident_loaded = sem("ident_loaded")
        vec_loaded = sem("vec_loaded")
        had_loaded = sem("had_loaded")
        const_made = sem("const_made")
        decay_made = sem("decay_made")
        x0_loaded = [sem(f"x0_loaded{i}") for i in range(TT)]
        w2_loaded = [sem(f"w2_loaded{i}") for i in range(W2_LOADS)]
        raw_loaded = [sem(f"raw_loaded{i}") for i in range(RAW)]
        late_loaded = sem("late_loaded")
        unit_stored = [sem(f"unit_stored{i}") for i in range(RING)]
        x_loaded = counted("x_loaded", 16)
        res_loaded = counted("res_loaded", 16)
        out_stored = counted("out_stored", 16)
        slot_loaded = [counted(f"slot_loaded{i}", 16 * TURNS) for i in range(RING)]
        w2_psum = sem("w2_psum")
        w2_copied = sem("w2_copied")
        fly_dve = sem("fly_dve")
        fly_pool = sem("fly_pool")
        unit_hi = sem("unit_hi")
        lo_dve, lo_pool = sem("lo_dve"), sem("lo_pool")
        unit_done = counted("unit_done", NU)
        rkv_bank = counted("rkv_bank", 9)
        xt_psum = counted("xt_psum", KT)
        acc_tile = counted("acc_tile", TT - 1)
        kvr_ready = counted("kvr_ready", 12)
        mix_prev = counted("mix_prev", 12)
        mix_hi = counted("mix_hi", 12)
        xs_hi = counted("xs_hi", KT)
        xt_copied = counted("xt_copied", KT)
        wkv_exp = counted("wkv_exp", 16)
        gate_tanh = counted("gate_tanh", FT)
        hid_hi = counted("hid_hi", FT)
        att_hi = counted("att_hi", KT)
        mix_full = counted("mix_full", 12)
        mix_lo = counted("mix_lo", 12)
        xs_lo = counted("xs_lo", KT)
        exp_arg = counted("exp_arg", 16)
        hid_full = counted("hid_full", FT)
        hid_lo = counted("hid_lo", FT)
        att_full = counted("att_full", KT)
        att_lo = counted("att_lo", KT)
        out_ready = counted("out_ready", TT)
        var_ready = counted("var_ready", 1)
        xn_ready = counted("xn_ready", TT)
        shift_ready = counted("shift_ready", 1)
        vec_step = sem("vec_step")
        rstd_ready = counted("rstd_ready", 1)

        def wait(eng, s, t, k):
            value = t * per[s.name] + k
            if not isinstance(value, int) or value > 0:
                eng.wait_ge(s, value)

        def wait_unit(eng, t, unit):
            wait(eng, unit_done, t, UNIT_AT[unit] + 1)

        def wait_item(eng, t, n):
            wait(eng, unit_done, t, n + 1 if n >= 0 else n + 13 - NU)

        block = ctx.enter_context(nc.Block())

        def over_chunks(eng, chunk):
            chunk(0)
            with eng.Fori(1, CHUNKS - 1) as t:
                chunk(t)
            chunk(CHUNKS - 1)

        def is_last(t):
            return isinstance(t, int) and t == CHUNKS - 1

        def place(unit):
            return resident[RESIDENT_AT[unit]] if unit in EARLY else ring[UNIT_AT[unit] % RING]

        def source(unit):
            return fly[1][:, unit[1], :] if unit[0] == "w2" else raw[RAW_ORDER.index(unit) % RAW][:, :]

        def wait_split(eng, unit):
            if unit in BY_POOL:
                eng.wait_ge(lo_pool, BY_POOL.index(unit) + 1)
            else:
                eng.wait_ge(lo_dve, BY_DVE.index(unit) + 1)

        @block.sync
        def _(sp):
            def rows(a, t):
                return a[bass.ds(t * N, N), :].rearrange("(t p) c -> p t c", p=P)

            def load_x(t):
                wait(sp, xt_psum, t - 1, KT)
                sp.dma_start(xn[:, :, :], rows(x, t)).then_inc(x_loaded, 16)

            def load_residual(t):
                wait(sp, out_stored, t - 1, 16)
                sp.dma_start(res[:, :, :], rows(x, t)).then_inc(res_loaded, 16)

            def store(t):
                wait(sp, out_ready, t, TT)
                sp.dma_start(rows(out, t), res[:, :, :]).then_inc(out_stored, 16)

            def load_raw(m):
                if m >= RAW:
                    wait_split(sp, RAW_ORDER[m - RAW])
                name, i = RAW_ORDER[m]
                sp.dma_start(raw[m % RAW][:, :], w_units[name][i]).then_inc(raw_loaded[m % RAW], 16)

            def wait_stored(unit):
                slot = UNIT_AT[unit] % RING
                sp.wait_ge(unit_stored[slot], 16 * len(in_slot(UNITS[:UNIT_AT[unit] + 1], slot)))

            def first_chunk():
                for n, unit in enumerate(UNITS):
                    wait_split(sp, unit)
                    if unit not in EARLY:
                        sp.dma_start(split[n].rearrange("p (a c) -> p a c", a=2),
                                     ring[n % RING][:, :, :].bitcast(f32)).then_inc(unit_stored[n % RING], 16)
                    if unit in RAW_ORDER and RAW_ORDER.index(unit) + RAW < len(RAW_ORDER):
                        load_raw(RAW_ORDER.index(unit) + RAW)
                    if unit == ("w1", 1):
                        load_x(1)
                    if unit == ("w1", 6):
                        load_residual(0)

            def chunk(t):
                second = isinstance(t, int) and t == 1
                for n, unit in enumerate(STREAMED):
                    if second and n < RING:
                        sp.wait_ge(unit_stored[n], 16 * len(in_slot(UNITS, n)))
                    if second:
                        wait_stored(unit)
                    if second and n < RING:
                        wait(sp, unit_done, 0, UNIT_AT[in_slot(UNITS, n)[-1]] + 1)
                    else:
                        wait(sp, unit_done, t, UNIT_AT[STREAMED[n - RING]] + 1 - (NU if n < RING else 0))
                    sp.dma_start(ring[n % RING][:, :, :].bitcast(f32),
                                 split[UNIT_AT[unit]].rearrange("p (a c) -> p a c", a=2))\
                        .then_inc(slot_loaded[n % RING], 16)
                    if second and n < len(RESIDENT) - len(EARLY):
                        late = RESIDENT[len(EARLY) + n]
                        wait_stored(late)
                        sp.dma_start(resident[len(EARLY) + n][:, :, :].bitcast(f32),
                                     split[UNIT_AT[late]].rearrange("p (a c) -> p a c", a=2))\
                            .then_inc(late_loaded, 16)
                    if n == 4 and not is_last(t):
                        load_x(t + 1)
                    if n == 9:
                        store(t - 1)
                    if n == 20:
                        load_residual(t)

            for tt in range(TT):
                sp.dma_start(xn[:, tt, :], x[tt * P:(tt + 1) * P, :]).then_inc(x0_loaded[tt], 16)
            sp.dma_start(vec[:, :, :], vectors).then_inc(vec_loaded, 16)
            sp.dma_start(ident[:, :], identity).then_inc(ident_loaded, 16)
            sp.dma_start(had[:, :], hadamard).then_inc(had_loaded, 16)
            for i in range(W2_LOADS):
                tiles = slice(i * FT // W2_LOADS, (i + 1) * FT // W2_LOADS)
                sp.dma_start(fly[0][:, tiles, :],
                             w_units["w2"][tiles].rearrange("j p c -> p j c")).then_inc(w2_loaded[i], 16)
            for m in range(RAW):
                load_raw(m)
            first_chunk()
            chunk(1)
            with sp.Fori(2, CHUNKS - 1) as t:
                chunk(t)
            chunk(CHUNKS - 1)
            for tt in range(TT):
                wait(sp, out_ready, CHUNKS - 1, tt + 1)
                row = (CHUNKS - 1) * N + tt * P
                sp.dma_start(out[row:row + P, :], res[:, tt, :]).then_inc(out_stored, 16)
            wait(sp, out_stored, CHUNKS - 1, 16 * TT)

        def butterflies(eng, done, half_stage, cols):
            stage, difference = divmod(half_stage, 2)
            h = 2 ** stage
            view = "p (g two h) c -> p g two h c"
            src, dst = (fly[(stage + i) % 2][:, :, :].rearrange(view, two=2, h=h) for i in (1, 0))
            if not difference:
                eng.wait_ge(done, 2 * stage)
            for g in range(FT // (2 * h)):
                last = eng.tensor_tensor(dst[:, g, difference, :, cols], src[:, g, 0, :, cols],
                                         src[:, g, 1, :, cols], ALU.subtract if difference else ALU.add)
            last.then_inc(done, 1)

        def first_butterfly(eng, done, j, cols):
            eng.wait_ge(w2_copied, j + 2)
            for i, op in enumerate((ALU.add, ALU.subtract)):
                last = eng.tensor_tensor(fly[0][:, j + i, cols], fly[1][:, j, cols],
                                         fly[1][:, j + 1, cols], op)
            if j == FT - 2:
                last.then_inc(done, 2)

        @block.gpsimd
        def _(pool):
            def inverse_root(t):
                wait(pool, var_ready, t, 1)
                pool.tensor_tensor(rstd[:, :], var_eps[:, :], half[:, :], ALU.pow).then_inc(rstd_ready, 1)

            pool.wait_ge(const_made, 1)
            inverse_root(0)
            for j in range(0, FT, 2):
                first_butterfly(pool, fly_pool, j, POOL_COLUMNS)
            for i in range(2, 8):
                butterflies(pool, fly_pool, i, POOL_COLUMNS)
            for i, unit in enumerate(BY_POOL):
                pool.wait_ge(unit_hi, UNIT_AT[unit] + 1)
                if unit == ("w2", 0):
                    pool.wait_ge(fly_dve, 8)
                    pool.wait_ge(fly_pool, 8)
                pool.tensor_tensor(place(unit)[:, 1, :], source(unit), place(unit)[:, 0, :].bitcast(f32),
                                   ALU.subtract).then_inc(lo_pool, 1)
                if unit == split_in_step(TT + 2)[0][-1]:
                    inverse_root(1)
            with pool.Fori(2, CHUNKS) as t:
                inverse_root(t)

        @block.tensor
        def _(pe):
            def weights(t, unit):
                if isinstance(t, int) and t == 0:
                    wait_split(pe, unit)
                    return place(unit)
                if unit in RESIDENT_AT:
                    if isinstance(t, int) and t == 1 and unit not in EARLY:
                        pe.wait_ge(late_loaded, 16 * (len(RESIDENT) - len(EARLY)))
                    return resident[RESIDENT_AT[unit]]
                n = STREAMED_AT[unit]
                wait(pe, slot_loaded[n % RING], t - 1, 16 * (n // RING + 1))
                return ring[n % RING]

            def transposes(t, kts, into):
                wait(pe, xn_ready, t, TT)
                for kt in kts:
                    for tt in range(TT):
                        last = pe.transpose(banks[into + kt % 2][:, tt * P:(tt + 1) * P],
                                            xn[:, tt, kt * P:(kt + 1) * P], ident[:, :])
                    last.then_inc(xt_psum, 1)

            def first_transposes():
                for tt in range(TT):
                    wait(pe, xn_ready, 0, tt + 1)
                    for kt in range(KT):
                        last = pe.transpose(banks[(kt + 2) % KT][:, tt * P:(tt + 1) * P],
                                            xn[:, tt, kt * P:(kt + 1) * P], ident[:, :])
                        if tt == TT - 1:
                            last.then_inc(xt_psum, 1)

            def rkv_item(t, n):
                q, kt = divmod(n, KT)
                w = weights(t, UNITS[n])
                m_in = mix[n % MIX_AHEAD]
                wait(pe, mix_hi, t, n + 1)
                wait(pe, mix_lo, t, n + 1)
                for m in range(KT):
                    if kt == 0:
                        if q == 0 and m % 2 == 0:
                            wait(pe, hid_full, t - 1, FT - 1 + m // 2)
                        elif q:
                            wait(pe, kvr_ready, t, KT * (q - 1) + m + 1)
                    col = slice(m * P, (m + 1) * P)
                    pe.matmul(banks[m][:, :], w[:, 0, col], m_in[:, 0, :], start=kt == 0, stop=False)
                    pe.matmul(banks[m][:, :], w[:, 1, col], m_in[:, 0, :], start=False, stop=False)
                    last = pe.matmul(banks[m][:, :], w[:, 0, col], m_in[:, 1, :], start=False,
                                     stop=kt == KT - 1)
                    if m == KT - 1:
                        last.then_inc(unit_done, 1)
                    elif kt == KT - 1:
                        last.then_inc(rkv_bank, 1)

            def up(t, j):
                b = 2 * (j % 2)
                if j == 0:
                    wait(pe, kvr_ready, t, 10)
                    wait(pe, xs_hi, t, KT)
                    wait(pe, xs_lo, t, KT)
                elif j == 1:
                    wait(pe, kvr_ready, t, 12)
                else:
                    wait(pe, hid_full, t, j - 1)
                if j in (FLIP_AT + 1, FLIP_AT + 2) and not is_last(t):
                    wait(pe, xt_copied, t + 1, 2 * (j - FLIP_AT))
                for n, name in enumerate(("w1", "w3")):
                    w = weights(t, (name, j))
                    for kt in range(KT):
                        col = slice(kt * P, (kt + 1) * P)
                        pe.matmul(banks[b + n][:, :], w[:, 0, col], xs[:, 0, kt, :], start=kt == 0, stop=False)
                        pe.matmul(banks[b + n][:, :], w[:, 1, col], xs[:, 0, kt, :], start=False, stop=False)
                        last = pe.matmul(banks[b + n][:, :], w[:, 0, col], xs[:, 1, kt, :], start=False,
                                         stop=kt == KT - 1)
                    last.then_inc(unit_done, 1)

            def down(t, unit, a, first=False, final=False):
                w = weights(t, unit)
                for tt in range(TT):
                    col = slice(tt * P, (tt + 1) * P)
                    if first:
                        wait(pe, out_ready, t - 1, tt + 1)
                    pe.matmul(acc[tt][:, :], a[:, 0, col], w[:, 0, :], start=first, stop=False)
                    pe.matmul(acc[tt][:, :], a[:, 1, col], w[:, 0, :], start=False, stop=False)
                    last = pe.matmul(acc[tt][:, :], a[:, 0, col], w[:, 1, :], start=False, stop=final)
                    if tt == TT - 1:
                        last.then_inc(unit_done, 1)
                    elif final:
                        last.then_inc(acc_tile, 1)

            def ffn_down(t, j):
                wait(pe, hid_hi, t, j + 1)
                wait(pe, hid_lo, t, j + 1)
                down(t, ("w2", j), hid[j % HID_SLOTS], first=j == 0, final=j == FT - 1)

            def att_down(t, c):
                wait(pe, att_hi, t, c + 1)
                wait(pe, att_lo, t, c + 1)
                down(t, ("wo", c), att[c % 2])

            def chunk(t):
                for n in range(12):
                    rkv_item(t, n)
                for j in range(FT):
                    up(t, j)
                    if j in (FLIP_AT, FLIP_AT + 1) and not is_last(t):
                        wait(pe, hid_full, t, j)
                        transposes(t + 1, (0, 1) if j == FLIP_AT else (2, 3), 2 - 2 * (j % 2))
                    if j >= LAG:
                        ffn_down(t, j - LAG)
                    if j >= 5 and j % 4 == 1:
                        att_down(t, (j - 5) // 4)
                ffn_down(t, FT - 2)
                att_down(t, KT - 1)
                ffn_down(t, FT - 1)

            pe.wait_ge(ident_loaded, 16)
            first_transposes()
            pe.wait_ge(had_loaded, 16)
            for j in range(FT):
                pe.wait_ge(w2_loaded[j * W2_LOADS // FT], 16)
                if j >= TT:
                    pe.wait_ge(w2_copied, j + 1 - TT)
                pe.matmul(acc[j % TT][:, :], had[:, :], fly[0][:, j, :], start=True, stop=True).then_inc(w2_psum, 1)
            over_chunks(pe, chunk)

        @block.scalar
        def _(act):
            def mix_first(t, n):
                q, kt = divmod(n, KT)
                if n == 0:
                    wait(act, xt_copied, t, KT)
                    wait(act, shift_ready, t, 1)
                wait(act, mix_lo, t, n + 1 - MIX_AHEAD)
                act.activation(mixf[n % MIX_AHEAD][:, :], xt[:, kt, 0:N], ACT.Copy,
                               scale=one_less_mu[:, q, kt:kt + 1]).then_inc(mix_prev, 1)

            def mix_second(t, n):
                wait(act, mix_full, t, n + 1)
                wait_item(act, t, n - MIX_AHEAD)
                act.activation(mix[n % MIX_AHEAD][:, 0, :], mixf[n % MIX_AHEAD][:, :],
                               ACT.Copy).then_inc(mix_hi, 1)

            def evacuate(t, q):
                for m in range(KT):
                    if m < KT - 1:
                        wait(act, rkv_bank, t, 3 * q + m + 1)
                    else:
                        wait_item(act, t, 4 * q + 3)
                    if q == 0 and m == 0:
                        wait(act, att_full, t - 1, KT)
                    act.activation(kvr[:, q, m, :], banks[m][:, :], ACT.Tanh if q == 2 else ACT.Copy,
                                   scale=0.5 if q == 2 else 1.0).then_inc(kvr_ready, 1)

            def copy_xt(t, kts, bank):
                wait(act, shift_ready, t, 1)
                for kt in kts:
                    wait(act, xt_psum, t, kt + 1)
                    act.activation(xt[:, kt, 1:N + 1], banks[bank + kt % 2][:, :],
                                   ACT.Copy).then_inc(xt_copied, 1)

            def split_hi(unit):
                n = UNIT_AT[unit]
                if unit[0] == "w2":
                    act.wait_ge(fly_dve, 8)
                    act.wait_ge(fly_pool, 8)
                else:
                    m = RAW_ORDER.index(unit)
                    act.wait_ge(raw_loaded[m % RAW], 16 * (m // RAW + 1))
                before = in_slot(UNITS[:n], n % RING)
                if unit not in EARLY and before:
                    act.wait_ge(unit_done, UNIT_AT[before[-1]] + 1)
                    act.wait_ge(unit_stored[n % RING], 16 * len(before))
                act.activation(place(unit)[:, 0, :], source(unit), ACT.Copy).then_inc(unit_hi, 1)

            def exponentials(t, c):
                for i, a in enumerate((0, 1, 4, 5)):
                    wait(act, exp_arg, t, 4 * c + i + 1)
                    act.activation(tmp[a][:, :], tmp[a][:, :], ACT.Exp).then_inc(wkv_exp, 1)

            def xs_first(kt):
                act.activation(xs[:, 0, kt, :], xt[:, kt, 1:N + 1], ACT.Copy).then_inc(xs_hi, 1)

            def chunk(t):
                first = isinstance(t, int) and t == 0
                if not first:
                    wait(act, unit_done, t, UNIT_AT[("w3", FT - 1)] + 1 - NU)
                    for kt in range(KT):
                        xs_first(kt)
                mix_first(t, MIX_AHEAD)
                for n in range(12):
                    if n % KT == KT - 1:
                        evacuate(t, n // KT)
                    if n + MIX_AHEAD < 12:
                        mix_second(t, n + MIX_AHEAD)
                    if n + MIX_AHEAD + 1 < 12:
                        mix_first(t, n + MIX_AHEAD + 1)
                    if first and n < 10:
                        split_hi(UNITS[n + SPLIT_AHEAD])
                if first:
                    for unit in units_of_step(1):
                        split_hi(unit)
                else:
                    exponentials(t, 0)
                for j in range(FT):
                    f = hidf[j % HID_SLOTS]
                    wait_unit(act, t, ("w1", j))
                    wait(act, hid_lo, t, j + 1 - HID_SLOTS)
                    act.activation(f[:, :], banks[2 * (j % 2)][:, :], ACT.Tanh, scale=0.5)\
                        .then_inc(gate_tanh, 1)
                    if first:
                        for unit in split_in_step(j)[0]:
                            split_hi(unit)
                        if j == 0:
                            exponentials(t, 0)
                    if j in (FLIP_AT, FLIP_AT + 1) and not is_last(t):
                        copy_xt(t + 1, (0, 1) if j == FLIP_AT else (2, 3), 2 - 2 * (j % 2))
                    wait(act, hid_full, t, j + 1)
                    wait(act, unit_done, t, UNIT_AT[("w2", (j - HID_SLOTS) % FT)] + 1
                         - (NU if j < HID_SLOTS else 0))
                    act.activation(hid[j % HID_SLOTS][:, 0, :], f[:, :], ACT.Copy).then_inc(hid_hi, 1)
                    if first:
                        for unit in split_in_step(j)[1]:
                            split_hi(unit)
                    c, stage = divmod(j + 1, 4)
                    if stage == 0 and c < KT:
                        exponentials(t, c)
                    if stage == 3:
                        wait(act, att_full, t, c + 1)
                        wait(act, unit_done, t, UNIT_AT[("wo", (c - 2) % KT)] + 1 - (NU if c < 2 else 0))
                        act.activation(att[c % 2][:, 0, :], tmp[6][:, :], ACT.Copy).then_inc(att_hi, 1)
                if not is_last(t):
                    mix_first(t + 1, 0)
                    for n in range(MIX_AHEAD):
                        if n + 1 < MIX_AHEAD:
                            mix_first(t + 1, n + 1)
                        mix_second(t + 1, n)

            act.wait_ge(vec_loaded, 16)
            act.activation(exp_w[:, :], vec[:, 3, :], ACT.Exp).then_inc(decay_made, 1)
            act.wait_ge(decay_made, 1)
            act.activation(decay[:, :], exp_w[:, :], ACT.Copy, scale=-1.0).then_inc(decay_made, 1)
            act.wait_ge(const_made, 2)
            copy_xt(0, (0, 1), 2)
            copy_xt(0, (2, 3), 0)
            mix_first(0, 0)
            for j in range(FT):
                act.wait_ge(w2_psum, j + 1)
                act.activation(fly[1][:, j, :], acc[j % TT][:, :], ACT.Copy,
                               scale=0.5 / float(np.sqrt(H))).then_inc(w2_copied, 1)
                if j < MIX_AHEAD:
                    if j + 1 < MIX_AHEAD:
                        mix_first(0, j + 1)
                    mix_second(0, j)
                elif 4 <= j < 4 + KT:
                    xs_first(j - 4)
                elif 4 + KT <= j < 4 + KT + SPLIT_AHEAD:
                    split_hi(UNITS[j - 4 - KT])
            over_chunks(act, chunk)

        @block.vector
        def _(dve):
            steps = [0, 0]

            def step(ins):
                steps[0] += 1
                ins.then_inc(vec_step, 1)
                return steps[0]

            def wait_step(base, k):
                dve.wait_ge(vec_step, base + k)

            def token_stats(t, tt):
                if isinstance(t, int) and t == 0:
                    dve.wait_ge(x0_loaded[tt], 16)
                elif tt == 0:
                    wait(dve, x_loaded, t - 1, 16)
                return step(dve.bn_stats(stats[:, tt, :], xn[:, tt, :]))

            def token_mean_var(tt):
                return step(dve.bn_aggr(mean_var[:, tt, :], stats[:, tt, :]))

            def add_eps(base, ready):
                wait_step(base, ready)
                dve.tensor_scalar(var_eps[:, :], mean_var[:, :, 1], EPS, None, ALU.add).then_inc(var_ready, 1)

            def normalise(t, tt):
                wait(dve, rstd_ready, t, 1)
                dve.tensor_scalar(xn[:, tt, :], xn[:, tt, :], mean_var[:, tt, 0:1], rstd[:, tt:tt + 1],
                                  ALU.subtract, ALU.mult).then_inc(xn_ready, 1)

            def mix_item(t, n):
                q, kt = divmod(n, KT)
                f = mixf[n % MIX_AHEAD]
                wait(dve, mix_prev, t, n + 1)
                dve.scalar_tensor_tensor(f[:, :], xt[:, kt, 1:N + 1], vec[:, q, kt:kt + 1], f[:, :],
                                         ALU.mult, ALU.add).then_inc(mix_full, 1)

            def mix_rest(t, n):
                f, m = mixf[n % MIX_AHEAD], mix[n % MIX_AHEAD]
                wait(dve, mix_hi, t, n + 1)
                dve.tensor_tensor(m[:, 1, :], f[:, :], m[:, 0, :].bitcast(f32), ALU.subtract)\
                    .then_inc(mix_lo, 1)

            def mix_items(t, first, end):
                mix_item(t, first)
                for n in range(first + 1, end):
                    mix_item(t, n)
                    mix_rest(t, n - 1)
                mix_rest(t, end - 1)

            def xs_rest(t, kt):
                wait(dve, xs_hi, t, kt + 1)
                dve.tensor_tensor(xs[:, 1, kt, :], xt[:, kt, 1:N + 1],
                                  xs[:, 0, kt, :].bitcast(f32), ALU.subtract).then_inc(xs_lo, 1)

            def shift(t):
                dve.tensor_scalar(xt[:, :, 0:1], xt[:, :, N:N + 1],
                                  keep[:, bass.ds(t, 1)], None, ALU.mult).then_inc(shift_ready, 1)

            def wkv(t, base, c, stage, at):
                k, v, th = (kvr[:, q, c, :] for q in range(3))
                before = [pab[:, i, 0:N] for i in range(3)]
                after = [pab[:, i, 1:N + 1] for i in range(3)]
                w, u = decay[:, c:c + 1], vec[:, 4, c:c + 1]
                if stage == 0:
                    if c == 0:
                        wait(dve, kvr_ready, t, 12)
                    step(dve.tensor_copy(pab[:, :, 0], carry[:, c, :]))
                    top = step(dve.tensor_tensor_scan(after[0], w.to_broadcast([P, N]), k,
                                                      carry[:, c, 0:1], ALU.add, ALU.max))
                    wait_step(base, top)
                    dve.scalar_tensor_tensor(tmp[0][:, :], before[0], w, after[0], ALU.add,
                                             ALU.subtract).then_inc(exp_arg, 1)
                    peak = step(dve.scalar_tensor_tensor(tmp[3][:, :], k, u, before[0], ALU.add, ALU.max))
                    dve.tensor_tensor(tmp[1][:, :], k, after[0], ALU.subtract).then_inc(exp_arg, 1)
                    wait_step(base, peak)
                    dve.tensor_tensor(tmp[4][:, :], before[0], tmp[3][:, :], ALU.subtract).then_inc(exp_arg, 1)
                    dve.scalar_tensor_tensor(tmp[5][:, :], k, u, tmp[3][:, :], ALU.add,
                                             ALU.subtract).then_inc(exp_arg, 1)
                elif stage == 1:
                    wait(dve, wkv_exp, t, 4 * c + 4)
                    ev = step(dve.tensor_tensor(tmp[2][:, :], tmp[1][:, :], v, ALU.mult))
                    at["den"] = step(dve.tensor_tensor_scan(after[2], tmp[0][:, :], tmp[1][:, :],
                                                            carry[:, c, 2:3], ALU.mult, ALU.add))
                    wait_step(base, ev)
                    at["num"] = step(dve.tensor_tensor_scan(after[1], tmp[0][:, :], tmp[2][:, :],
                                                            carry[:, c, 1:2], ALU.mult, ALU.add))
                    at["ev"] = step(dve.tensor_tensor(tmp[3][:, :], tmp[5][:, :], v, ALU.mult))
                elif stage == 2:
                    wait_step(base, at["ev"])
                    d = step(dve.tensor_tensor(tmp[2][:, :], tmp[4][:, :], before[2], ALU.mult))
                    n = step(dve.tensor_tensor(tmp[6][:, :], tmp[4][:, :], before[1], ALU.mult))
                    wait_step(base, d)
                    at["d"] = step(dve.tensor_tensor(tmp[2][:, :], tmp[2][:, :], tmp[5][:, :], ALU.add))
                    wait_step(base, n)
                    at["n"] = step(dve.tensor_tensor(tmp[6][:, :], tmp[6][:, :], tmp[3][:, :], ALU.add))
                else:
                    wait_step(base, at["n"])
                    r = step(dve.reciprocal(tmp[2][:, :], tmp[2][:, :]))
                    kept = step(dve.tensor_tensor(carry_kept[:, :], pab[:, :, N],
                                                  keep3[:, bass.ds(t * 3 + 3, 3)], ALU.mult))
                    wait_step(base, r)
                    y = step(dve.scalar_tensor_tensor(tmp[6][:, :], tmp[6][:, :], 0.5, tmp[2][:, :],
                                                      ALU.mult, ALU.mult))
                    wait_step(base, kept)
                    step(dve.tensor_tensor(carry[:, c, :], carry_kept[:, :],
                                           reset3[:, bass.ds(t * 3 + 3, 3)], ALU.add))
                    wait_step(base, y)
                    dve.scalar_tensor_tensor(tmp[6][:, :], th, 1.0, tmp[6][:, :], ALU.add,
                                             ALU.mult).then_inc(att_full, 1)

            def att_rest(t, c):
                wait(dve, att_hi, t, c + 1)
                dve.tensor_tensor(att[c % 2][:, 1, :], tmp[6][:, :], att[c % 2][:, 0, :].bitcast(f32),
                                  ALU.subtract).then_inc(att_lo, 1)

            def split_lo(unit):
                dve.wait_ge(unit_hi, UNIT_AT[unit] + 1)
                dve.tensor_tensor(place(unit)[:, 1, :], source(unit), place(unit)[:, 0, :].bitcast(f32),
                                  ALU.subtract).then_inc(lo_dve, 1)

            def chunk(t):
                steps[0] = 0
                first = isinstance(t, int) and t == 0
                base = t * STEPS + steps[1]
                at = {}
                if not first:
                    wait_step(base, 0)
                mix_item(t, MIX_AHEAD)
                for n in range(MIX_AHEAD, 12):
                    if n + 1 < 12:
                        mix_item(t, n + 1)
                    mix_rest(t, n)
                    if n == 10 and not first:
                        for kt in range(KT):
                            xs_rest(t, kt)
                    if first:
                        split_lo(UNITS[n + SPLIT_AHEAD - MIX_AHEAD])
                        if n > 3 and n % 3:
                            butterflies(dve, fly_dve, 2 * (n // 3) + n % 3 - 1, DVE_COLUMNS)
                if first:
                    split_lo(UNITS[LO_BY_DVE - 1])
                    dve.wait_ge(fly_pool, 8)
                    dve.wait_ge(fly_dve, 8)
                wkv(t, base, 0, 0, at)
                for j in range(FT):
                    f, h, b = hidf[j % HID_SLOTS], hid[j % HID_SLOTS], 2 * (j % 2)
                    wait(dve, gate_tanh, t, j + 1)
                    g = step(dve.scalar_tensor_tensor(f[:, :], f[:, :], 1.0, banks[b][:, :], ALU.add, ALU.mult))
                    wait_unit(dve, t, ("w3", j))
                    wait_step(base, g)
                    dve.tensor_tensor(f[:, :], f[:, :], banks[b + 1][:, :], ALU.mult).then_inc(hid_full, 1)
                    c, stage = divmod(j + 1, 4)
                    if stage == 0:
                        att_rest(t, c - 1)
                    if c < KT:
                        wkv(t, base, c, stage, at)
                    if not is_last(t):
                        if 1 < j <= TT + 1:
                            at["mean_var"] = token_mean_var(j - 2)
                        if 1 <= j <= TT:
                            token_stats(t + 1, j - 1)
                        if j == TT + 2:
                            add_eps(base, at["mean_var"])
                        if TT + 3 <= j < 2 * TT + 3:
                            normalise(t + 1, j - TT - 3)
                        if j == 2 * TT + 3:
                            shift(t + 1)
                    wait(dve, hid_hi, t, j + 1)
                    dve.tensor_tensor(h[:, 1, :], f[:, :], h[:, 0, :].bitcast(f32), ALU.subtract)\
                        .then_inc(hid_lo, 1)
                if not is_last(t):
                    mix_items(t + 1, 0, MIX_AHEAD)
                wait(dve, res_loaded, t, 16)
                for tt in range(TT):
                    if tt < TT - 1:
                        wait(dve, acc_tile, t, tt + 1)
                    else:
                        wait(dve, unit_done, t, NU)
                    dve.tensor_tensor(res[:, tt, :], res[:, tt, :], acc[tt][:, :], ALU.add)\
                        .then_inc(out_ready, 1)
                if not is_last(t):
                    assert steps[0] == STEPS, steps

            dve.memset(half[:, :], -0.5).then_inc(const_made, 1)
            for table, value in ((keep, 1.0), (keep3, 1.0), (reset3, 0.0), (carry, 0.0)):
                at0 = step(dve.memset(table[:], value))
            wait_step(0, at0)
            rows = CHUNKS_PER_ROW
            step(dve.memset(keep[:, 0:CHUNKS + 1:rows], 0.0))
            step(dve.memset(keep3[:, :].rearrange("p (s a) -> p s a", a=3)[:, 0:CHUNKS + 1:rows, :], 0.0))
            step(dve.memset(reset3[:, :].rearrange("p (s a) -> p s a", a=3)[:, 0:CHUNKS + 1:rows, 0], START))
            step(dve.memset(carry[:, :, 0], START))
            for tt in range(TT):
                wait_step(0, token_stats(0, tt))
                done = token_mean_var(tt)
            add_eps(0, done)
            dve.wait_ge(vec_loaded, 16)
            dve.tensor_scalar(one_less_mu[:, :, :], vec[:, 0:3, :], -1.0, 1.0, ALU.mult, ALU.add)\
                .then_inc(const_made, 1)
            dve.wait_ge(decay_made, 2)
            for tt in range(TT):
                normalise(0, tt)
            dve.memset(xt[:, :, 0], 0.0).then_inc(shift_ready, 1)
            steps[1] = steps[0]
            mix_items(0, 0, MIX_AHEAD)
            for j in range(0, FT, 2):
                first_butterfly(dve, fly_dve, j, DVE_COLUMNS)
                if j in (4, 6):
                    xs_rest(0, j - 4)
                    xs_rest(0, j - 3)
                if j in (8, 10):
                    split_lo(UNITS[j - 8])
                    split_lo(UNITS[j - 7])
            over_chunks(dve, chunk)


STEPS = 15 * KT + FT + 2 * TT


def _square_units(w):
    return np.ascontiguousarray(w.T).reshape(KT, P, C)


def _up_units(w):
    return np.ascontiguousarray(w.reshape(FT, P, KT, P).transpose(0, 3, 2, 1)).reshape(FT, P, KT * P)


def kernel(L0_attn_x, L0_attn_mu_r, L0_attn_mu_k, L0_attn_mu_v, L0_attn_wkv_w, L0_attn_wkv_u,
           L0_attn_Wr, L0_attn_Wk, L0_attn_Wv, L0_attn_Wo, L0_ffn_W1, L0_ffn_W2, L0_ffn_W3):
    import concourse.bacc as bacc
    from concourse.bass_utils import run_bass_kernel_spmd

    weights = {
        "k": _square_units(np.asarray(L0_attn_Wk)), "v": _square_units(np.asarray(L0_attn_Wv)),
        "r": _square_units(np.asarray(L0_attn_Wr)), "wo": _square_units(np.asarray(L0_attn_Wo)),
        "w1": _up_units(np.asarray(L0_ffn_W1)), "w3": _up_units(np.asarray(L0_ffn_W3)),
        "w2": np.ascontiguousarray(np.asarray(L0_ffn_W2).T).reshape(FT, P, C),
    }
    vectors = np.stack([np.asarray(v).reshape(KT, P).T for v in
                        (L0_attn_mu_k, L0_attn_mu_v, L0_attn_mu_r, L0_attn_wkv_w, L0_attn_wkv_u)], axis=1)
    hadamard = np.ones((1, 1), np.float32)
    while len(hadamard) < P:
        hadamard = np.block([[hadamard, hadamard], [hadamard, -hadamard]])
    arrays = {
        "x": np.ascontiguousarray(np.asarray(L0_attn_x).reshape(B * T, C)),
        "vectors": np.ascontiguousarray(vectors),
        "hadamard": np.ascontiguousarray(hadamard, np.float32),
        "identity": np.eye(P, dtype=np.float32),
    } | {f"units_{n}": w for n, w in weights.items()}

    nc = bacc.Bacc("TRN2", target_bir_lowering=False, num_devices=1)
    ap = {n: nc.dram_tensor(n, a.shape, mybir.dt.from_np(a.dtype), kind="ExternalInput").ap()
          for n, a in arrays.items()}
    out = nc.dram_tensor("out", (B * T, C), mybir.dt.float32, kind="ExternalOutput").ap()
    build(nc, ap["x"], {n: ap[f"units_{n}"] for n in weights}, ap["vectors"], ap["hadamard"],
          ap["identity"], out)
    r = run_bass_kernel_spmd(nc, [arrays], core_ids=[0])
    return r.results[0]["out"].reshape(B, T, C)
```
